# Optimizing a Trainium2 kernel written in Bass

```python
import numpy as np
import jax
import jax.numpy as jnp

def _softmax(x, axis=-1):
    return jax.nn.softmax(x, axis=axis)

def _gelu(x):
    return jax.nn.gelu(x, approximate=True)

def _silu(x):
    return jax.nn.silu(x)

def _sigmoid(x):
    return jax.nn.sigmoid(x)

def _layernorm(x, axis=-1, eps=1e-05):
    m = jnp.mean(x, axis=axis, keepdims=True)
    v = jnp.var(x, axis=axis, keepdims=True)
    return (x - m) / jnp.sqrt(v + eps)

def _scatter_add(tgt, idx, src, axis=0):
    return tgt.at[idx].add(src)

def _segment_sum(src, seg, n):
    return jax.ops.segment_sum(src, seg, n)
kernel_name = 'mk_gnn_resnorm_d1_gnn_r8_3e2c7a'

def setup_inputs(seed: int=0):
    np.random.seed(seed)
    _w = jnp.asarray

    def _rec_inputs():
        import jax
        import jax.numpy as jnp
        _gk = jax.random.key(seed)
        x = -0.000202 + 1 * jax.random.normal(jax.random.fold_in(_gk, 1), (12500, 128), jnp.float32)
        _s = jax.random.randint(jax.random.fold_in(_gk, 2), (200000,), 0, 12500, jnp.int32)
        _d = jax.random.randint(jax.random.fold_in(_gk, 3), (200000,), 0, 12500, jnp.int32)
        _loop = jnp.arange(12500, dtype=jnp.int32)
        src = jnp.concatenate([_s, _d, _loop])
        dst = jnp.concatenate([_d, _s, _loop])
        _o = jnp.argsort(dst, stable=True)
        src = src[_o]
        dst = dst[_o]
        return (x, src, dst)
    x, src, dst = _rec_inputs()

    def _L0_gnn_setup():
        import jax, jax.numpy as jnp
        import numpy as np
        N_NODES = 6250
        N_EDGES = 100000
        DIM = 128
        ATTN_DIM = 64
        key = jax.random.key(seed)
        ks = jax.random.split(key, 8)
        X = jax.random.normal(ks[0], (N_NODES, DIM), dtype=jnp.float32)
        edge_index = jax.random.randint(ks[1], (2, N_EDGES), 0, N_NODES, dtype=jnp.int64)
        s = 1.0 / np.sqrt(DIM)
        sa = 1.0 / np.sqrt(ATTN_DIM)
        Wq = jax.random.uniform(ks[2], (DIM, ATTN_DIM), jnp.float32, -s, s)
        Wk = jax.random.uniform(ks[3], (DIM, ATTN_DIM), jnp.float32, -s, s)
        Wphi = jax.random.uniform(ks[4], (ATTN_DIM,), jnp.float32, -sa, sa)
        Wy_w = jax.random.uniform(ks[5], (DIM, DIM), jnp.float32, -s, s)
        Wy_b = jax.random.uniform(ks[6], (DIM,), jnp.float32, -s, s)
        We = jax.random.uniform(ks[7], (ATTN_DIM, DIM), jnp.float32, -sa, sa)
        return {'X': X, 'edge_index': edge_index, 'Wq': Wq, 'Wk': Wk, 'Wphi': Wphi, 'Wy_w': Wy_w, 'Wy_b': Wy_b, 'We': We}
    _L0_gnn_all = _L0_gnn_setup()
    _L0_gnn_in = {k: v for k, v in _L0_gnn_all.items() if k in ('Wq', 'Wk', 'Wphi', 'Wy_w', 'Wy_b', 'We')}
    del _L0_gnn_all
    return {'x': x, 'src': src, 'dst': dst, 'L0_gnn_Wq': _L0_gnn_in['Wq'], 'L0_gnn_Wk': _L0_gnn_in['Wk'], 'L0_gnn_Wphi': _L0_gnn_in['Wphi'], 'L0_gnn_Wy_w': _L0_gnn_in['Wy_w'], 'L0_gnn_Wy_b': _L0_gnn_in['Wy_b'], 'L0_gnn_We': _L0_gnn_in['We']}

def reference(x, src, dst, L0_gnn_Wq, L0_gnn_Wk, L0_gnn_Wphi, L0_gnn_Wy_w, L0_gnn_Wy_b, L0_gnn_We):
    import jax
    import jax.numpy as jnp

    def _L0_gnn_ref(X, edge_index, Wq, Wk, Wphi, Wy_w, Wy_b, We):
        import jax, jax.numpy as jnp
        import numpy as np
        N_NODES = 6250
        N_EDGES = 100000
        DIM = 128
        ATTN_DIM = 64
        N = X.shape[0]
        src, dst = (edge_index[0], edge_index[1])
        q = (X @ Wq)[src]
        k = (X @ Wk)[dst]
        e = jnp.tanh(q + k)
        scores = e @ Wphi
        scores = scores - jnp.max(scores)
        exp_scores = jnp.exp(scores)
        denom = jax.ops.segment_sum(exp_scores, src, num_segments=N)
        alpha = exp_scores / (denom[src] + 1e-09)
        vy = (X @ Wy_w + Wy_b)[dst]
        ve = e @ We
        msg = alpha[:, None] * (vy + ve)
        out = jax.ops.segment_sum(msg, src, num_segments=N)
        return out
    edge_index = jnp.stack([src, dst])
    x = _layernorm(x + _L0_gnn_ref(x, edge_index, L0_gnn_Wq, L0_gnn_Wk, L0_gnn_Wphi, L0_gnn_Wy_w, L0_gnn_Wy_b, L0_gnn_We), axis=-1)
    return x

_drawn_inputs = setup_inputs


def setup_inputs(seed=0):
    import zlib

    import numpy as np

    out = dict(_drawn_inputs(seed))
    spreads = {}
    factors = {}
    for name, (base, spread) in spreads.items():
        noise = np.random.default_rng([zlib.crc32(name.encode()), seed]).standard_normal(out[name].shape)
        drawn = base * np.exp(spread * noise) if base else spread * noise
        out[name] = jnp.asarray(drawn.astype(out[name].dtype))
    for name, factor in factors.items():
        out[name] = (out[name] * factor).astype(out[name].dtype)
    return out
```

```python
import concourse.bass as bass
from concourse import mybir
from contextlib import ExitStack

PARTS = 128
UNIT = 8
PAIR = 2
UNITS_PER_PAIR = PAIR * PARTS // UNIT
UNITS_PER_ROW = PARTS // UNIT
CHUNK = 16
PAIRS_PER_CHUNK = CHUNK // PAIR
LOOSE_BOUND = 30.0
FAR = 65536.0
SKIP = float(1 << 21)


class Counter:

    def __init__(self, sem):
        self.sem, self.value = sem, 0

    def add(self, by):
        self.value += by
        return (self, self.value)


class Queue:

    def __init__(self):
        self.items, self.reached = [], {}

    def put(self, build, waits=(), done=None, by=1):
        need = []
        for counter, value in waits:
            if self.reached.get(counter, 0) < value:
                self.reached[counter] = value
                need.append((counter.sem, value))
        self.items.append((need, build, done.sem if done else None, by))
        return done.add(by) if done else None

    def run(self, engine):
        for need, build, sem, by in self.items:
            for s, value in need:
                engine.wait_ge(s, value)
            made = build(engine) if build else None
            if sem is not None:
                made.then_inc(sem, by)
        self.items = []


def gnn_program(nc, x, src, dst, Wq, Wk, Wphi, Wy_w, Wy_b, We, out):
    f32, i32, u32 = mybir.dt.float32, mybir.dt.int32, mybir.dt.uint32
    bf16, f16 = mybir.dt.bfloat16, mybir.dt.float16
    ALU, ACT, AX = mybir.AluOpType, mybir.ActivationFunctionType, mybir.AxisListType

    N, D = x.shape
    E = src.shape[0]
    A = Wq.shape[1]
    NB = -(-N // PARTS)
    LAST = N - (NB - 1) * PARTS
    NT = -(-E // PARTS)
    EW = E // PARTS
    EREST = E - EW * PARTS
    ROW = A + D
    SUMS = D + A + 1
    SLOT = ROW + A + 1

    TPG = min(NT, (PARTS * PARTS - NB * (UNIT - 1)) // PARTS)
    NG = -(-NT // TPG)
    g_tiles = [min(TPG, NT - g * TPG) for g in range(NG)]
    max_units = (E + NG * NB * (UNIT - 1)) // UNIT
    max_pairs = (max_units + NB * (UNITS_PER_PAIR - 1)) // UNITS_PER_PAIR
    NP = -(-max_pairs // PAIRS_PER_CHUNK) * PAIRS_PER_CHUNK
    NTS = NP * PAIR
    LU = NTS * UNITS_PER_ROW
    MAPC = 16
    assert NP <= PARTS * MAPC and N + 1 < 1 << 14 and NB * (UNIT - 1) < PARTS * PARTS // 2
    HC = 30
    PB = 512 // NB
    GB = 4

    table = nc.dram_tensor("table", (N + 1, ROW), f32).ap()
    slist = nc.dram_tensor("sorted_list", (LU, UNIT), i32).ap()

    ctx = ExitStack()
    with ctx:
        def scope():
            return ExitStack()

        def sb(where, name, shape, dt):
            return where.enter_context(nc.sbuf_tensor(name, shape, dt))

        def sem(name):
            return Counter(ctx.enter_context(nc.semaphore(name)))

        bank = [ctx.enter_context(nc.psum_tensor(f"bank{i}", [PARTS, 512], f32)) for i in range(8)]

        row1 = sb(ctx, "row_1_to_128", [PARTS, PARTS], f32)
        part = sb(ctx, "partition_number", [PARTS, 1], f32)
        row1c = sb(ctx, "row_1_to_128_chunk", [PARTS, PARTS, CHUNK], bf16)
        identf = sb(ctx, "identity_f32", [PARTS, PARTS], f32)
        identb = sb(ctx, "identity_bf16", [PARTS, PARTS], bf16)
        before = sb(ctx, "before", [PARTS, PARTS], bf16)
        before_far = sb(ctx, "before_far", [PARTS, PARTS], bf16)
        ones = sb(ctx, "ones", [PARTS, PARTS], bf16)
        onesf = sb(ctx, "ones_f32", [1, PARTS], f32)
        pick = sb(ctx, "pick", [PARTS, 2 * TPG], bf16)
        wkq = sb(ctx, "wk_wq", [D, 2 * A], f32)
        wy = sb(ctx, "wy", [D, D], f32)
        web = sb(ctx, "we_bias", [A + 1, D], f32)
        phi = sb(ctx, "phi", [PARTS, A], f32)
        row0 = sb(ctx, "table_row_0", [1, ROW], f32)
        stat = sb(ctx, "stat", [PARTS, 8], f32)
        BOUND, NSHIFT, RMAX, GMAX, EPS9, TMP = (stat[:, i:i + 1] for i in range(6))
        passes = sb(ctx, "passes", [1, 1], i32)
        q3 = sb(ctx, "q_parts", [PARTS, NB * 3 * A], bf16)
        bmap = sb(ctx, "pair_blocks", [PARTS, 2, MAPC], i32)

        Q = {k: Queue() for k in ("sync", "gpsimd", "vector", "scalar", "tensor")}
        SP, PO, VE, AC, PE = (Q[k] for k in ("sync", "gpsimd", "vector", "scalar", "tensor"))
        po, ve, ac, pe = sem("pool_done"), sem("vector_done"), sem("scalar_done"), sem("tensor_done")
        fence_sems = {k: sem(f"fence_{k}") for k in Q}

        def V(build, *waits):
            return VE.put(build, [(ve, ve.value), *waits] if ve.value else waits, ve)

        def fence():
            for k, q in Q.items():
                q.put(lambda e: e.drain(), (), fence_sems[k])
            for k, q in Q.items():
                q.put(None, [(c, c.value) for j, c in fence_sems.items() if j != k])

        ld = sem("weights_loaded")
        for dst_ap, src_ap in ((wkq[:, 0:A], Wk), (wkq[:, A:2 * A], Wq), (wy[:, :], Wy_w),
                               (web[0:A, :], We), (web[A:A + 1, :], Wy_b.rearrange("(a n) -> a n", a=1)),
                               (phi[:, :], Wphi.rearrange("(a n) -> a n", a=1).to_broadcast([PARTS, A]))):
            loaded = SP.put(lambda e, d=dst_ap, s=src_ap: e.dma_start(d, s), (), ld, 16)
        tabx = sem("table_x_written")
        AC.put(lambda e: e.dma_start(table[1:N + 1, A:ROW], x), (), tabx, 16)

        PO.put(lambda e: e.iota(row1[:, :], [[1, PARTS]], base=1, channel_multiplier=0,
                                allow_small_or_imprecise_dtypes=True), (), po)
        PO.put(lambda e: e.iota(part[:, :], [[0, 1]], base=1, channel_multiplier=1,
                                allow_small_or_imprecise_dtypes=True), (), po)
        iotas = PO.put(lambda e: e.iota(row1c[:, :, :], [[1, PARTS], [0, CHUNK]], base=1, channel_multiplier=0,
                                        allow_small_or_imprecise_dtypes=True), (), po)
        V(lambda e: e.tensor_scalar(identf[:, :], row1[:, :], part[:, :], None, ALU.is_equal), iotas)
        V(lambda e: e.tensor_scalar(identb[:, :], row1[:, :], part[:, :], None, ALU.is_equal))
        V(lambda e: e.tensor_scalar(before[:, :], row1[:, :], part[:, :], None, ALU.is_gt))
        V(lambda e: e.scalar_tensor_tensor(before_far[:, :], identf[:, :], FAR, before[:, :], ALU.mult, ALU.add))
        V(lambda e: e.memset(ones[:, :], 1.0))
        V(lambda e: e.memset(onesf[:, :], 1.0))
        V(lambda e: e.memset(pick[:, :], 0.0))
        V(lambda e: e.memset(pick[:, TPG - 1:TPG], 1.0))
        V(lambda e: e.tensor_reduce(BOUND, phi[:, :], AX.X, ALU.add, apply_absolute_value=True), loaded)
        V(lambda e: e.tensor_scalar(NSHIFT, BOUND, -1.0, None, ALU.mult))
        V(lambda e: e.tensor_scalar(passes[:, :], BOUND[0:1, :], LOOSE_BOUND, 1.0, ALU.is_ge, ALU.add))
        V(lambda e: e.memset(row0[:, :], 0.0))
        V(lambda e: e.tensor_scalar(row0[:, 0:A], phi[0:1, :], 0.0, 60.0, ALU.is_lt, ALU.mult))
        row0_made = V(lambda e: e.tensor_scalar(row0[:, 0:A], row0[:, 0:A], -30.0, None, ALU.add))
        tab0 = sem("table_row_0_written")
        SP.put(lambda e: e.dma_start(table[0:1, :], row0[:, :]), (row0_made,), tab0, 16)

        nodes = scope()
        xin = sb(nodes, "x_in", [PARTS, 2, GB, D], f32)
        xT = sb(nodes, "xT", [PARTS, 2, GB * PARTS], f32)
        kst = sb(nodes, "k_and_q", [PARTS, 2, GB, 2 * A], f32)
        rest = sb(nodes, "q_rest", [PARTS, GB, A], f32)
        zeros = sb(nodes, "zero_units", [PARTS, LU // PARTS * UNIT], i32)
        zeroed = PO.put(lambda e: e.memset(zeros[:, :], 0), (), po)
        lz = sem("list_zeroed")
        AC.put(lambda e: e.dma_start(slist.rearrange("(p a) u -> p (a u)", p=PARTS), zeros[:, :]), (zeroed,), lz, 16)
        xl = [sem(f"x_loaded_{i}") for i in range(2)]
        ks = [sem(f"k_stored_{i}") for i in range(2)]
        q3v = q3[:, :].rearrange("p (b s f) -> p b s f", s=3, f=A)
        xT_free, xin_free, k_free = [None] * 2, [None] * 2, [None] * 2
        bankA_free, bankB_free, q_free = [None] * 2, [None] * 2, [None] * 2
        some = lambda *w: [z for z in w if z is not None]
        for i in range(-(-NB // GB)):
            s, b0 = i % 2, i * GB
            n = min(GB, NB - b0)
            whole = n if b0 + n < NB or LAST == PARTS else n - 1
            waits = some(xin_free[s])
            if whole < n:
                waits = [VE.put(lambda e, s=s, w=whole: e.memset(xin[:, s, w, :], 0.0), waits, ve)]
            got = None
            if whole:
                got = SP.put(lambda e, s=s, w=whole, b0=b0: e.dma_start(
                    xin[:, s, 0:w, :], x[b0 * PARTS:(b0 + w) * PARTS, :].rearrange("(b p) d -> p b d", p=PARTS)),
                    waits, xl[s], 16)
            if whole < n:
                got = SP.put(lambda e, s=s, w=whole: e.dma_start(
                    xin[0:LAST, s, w, :], x[(NB - 1) * PARTS:N, :]), waits, xl[s], 16)
            A_, B_ = bank[s], bank[2 + s]
            for j in range(n):
                t = PE.put(lambda e, j=j, s=s, A_=A_: e.transpose(A_[:, j * PARTS:(j + 1) * PARTS], xin[:, s, j, :], identf[:, :]),
                           some(got, bankA_free[s], (ve, ve.value)), pe)
            xin_free[s] = t
            bankA_free[s] = AC.put(lambda e, s=s, n=n, A_=A_: e.activation(xT[:, s, 0:n * PARTS], A_[:, 0:n * PARTS], ACT.Copy),
                                   some(t, xT_free[s]), ac)
            for j in range(n):
                t = PE.put(lambda e, j=j, s=s, B_=B_: e.matmul(B_[:, j * 2 * A:(j + 1) * 2 * A], xT[:, s, j * PARTS:(j + 1) * PARTS],
                                                               wkq[:, :], start=True, stop=True),
                           some(bankA_free[s], bankB_free[s], loaded), pe)
            xT_free[s] = t
            kq = B_[:, 0:n * 2 * A].rearrange("p (b c) -> p b c", c=2 * A)
            kdone = bankB_free[s] = AC.put(lambda e, s=s, n=n, kq=kq: e.activation(kst[:, s, 0:n, :], kq, ACT.Copy),
                                           some(t, k_free[s], q_free[s]), ac)
            qs = kst[:, s, 0:n, A:2 * A]
            out_rows = [(0, whole, PARTS)] * (whole > 0) + [(whole, 1, LAST)] * (whole < n)
            for w0, w, rows in out_rows:
                r0 = 1 + (b0 + w0) * PARTS
                k_free[s] = SP.put(lambda e, s=s, w0=w0, w=w, rows=rows, r0=r0: e.dma_start(
                    table[r0:r0 + (w - 1) * PARTS + rows, 0:A].rearrange("(b p) f -> p b f", p=rows),
                    kst[0:rows, s, w0:w0 + w, 0:A]), (kdone,), ks[s], 16)
            V(lambda e, qs=qs, b0=b0, n=n: e.tensor_copy(q3v[:, b0:b0 + n, 0, :], qs), kdone)
            V(lambda e, qs=qs, b0=b0, n=n: e.tensor_tensor(rest[:, 0:n, :], qs, q3v[:, b0:b0 + n, 0, :], ALU.subtract))
            V(lambda e, b0=b0, n=n: e.tensor_copy(q3v[:, b0:b0 + n, 1, :], rest[:, 0:n, :]))
            V(lambda e, b0=b0, n=n: e.tensor_tensor(rest[:, 0:n, :], rest[:, 0:n, :], q3v[:, b0:b0 + n, 1, :], ALU.subtract))
            q_free[s] = V(lambda e, b0=b0, n=n: e.tensor_copy(q3v[:, b0:b0 + n, 2, :], rest[:, 0:n, :]))
        SP.put(None, [(c, c.value) for c in (*xl, *ks)])
        AC.put(None, [(lz, 16)])
        fence()
        nodes.close()

        sort = scope()
        sortd = sb(sort, "sorted_groups", [PARTS, NG, PARTS], i32)
        dest = sb(sort, "unit_destinations", [PARTS, NG * UNITS_PER_ROW], i32)
        blk = sb(sort, "edge_block", [PARTS, NT], bf16)
        rec_hi = sb(sort, "record_high", [PARTS, NT], f16)
        rec_lo = sb(sort, "record_low", [PARTS, NT], f16)
        hot = sb(sort, "block_onehots", [PARTS, 2, -(-TPG // HC) * HC * NB], bf16)
        tmp = hot[:, 0, :].bitcast(i32)[:, 0:NT]
        rowbc = sb(sort, "row_0_to_nb_chunk", [PARTS, NB, HC], bf16)
        pos = sb(sort, "places", [PARTS, TPG], f32)
        posi = sb(sort, "places_int", [PARTS, TPG], i32)
        prc = sb(sort, "place_row_col_int", [PARTS, 2, TPG], i32)
        prow = sb(sort, "place_row", [PARTS, TPG], bf16)
        pcol = sb(sort, "place_col", [PARTS, TPG], bf16)
        cntb = sb(sort, "counts_bf16", [PARTS, NB], bf16)
        toti = sb(sort, "totals_int", [PARTS, NB], i32)
        basei = sb(sort, "base_int", [PARTS, 3, NB], i32)
        base = sb(sort, "base_parts", [PARTS, 2, NB], bf16)
        shi = sb(sort, "record_high_out", [PARTS, PARTS], f32)
        units = sb(sort, "run_units", [PARTS, NG, NB], f16)
        starts = sb(sort, "run_starts", [PARTS, NG, NB + 1], f16)
        raw = scope()
        srcs = sb(raw, "src_edges", [PARTS, NT], i32)
        dsts = sb(raw, "dst_edges", [PARTS, NT], i32)

        el = sem("edges_loaded")
        MANY = 1 << 20
        VE.put(lambda e: e.memset(srcs[:, EW:NT], MANY), (), ve) if EREST else None
        pads = VE.put(lambda e: e.memset(dsts[:, EW:NT], 0), (), ve) if EREST else None
        for t_, a_ in ((srcs, src), (dsts, dst)):
            SP.put(lambda e, t_=t_, a_=a_: e.dma_start(t_[:, 0:EW], a_[0:EW * PARTS].rearrange("(p c) -> p c", p=PARTS)), (), el, 16)
            if EREST:
                SP.put(lambda e, t_=t_, a_=a_: e.dma_start(t_[0:EREST, EW:NT], a_[EW * PARTS:E].rearrange("(p c) -> p c", c=1)), (pads,), el, 16)
        rows = PO.put(lambda e: e.iota(rowbc[:, :, :], [[1, NB], [0, HC]], base=0, channel_multiplier=0,
                                       allow_small_or_imprecise_dtypes=True), (), po)
        S_ = srcs[:, :]
        D_ = dsts[:, :]
        V(lambda e: e.tensor_scalar(tmp, S_, 7, None, ALU.logical_shift_right), (el, el.value))
        V(lambda e: e.tensor_copy(blk[:, :], tmp))
        V(lambda e: e.tensor_scalar(S_, S_, PARTS - 1, None, ALU.bitwise_and))
        V(lambda e: e.scalar_tensor_tensor(D_, D_, 256.0, S_, ALU.mult, ALU.add))
        V(lambda e: e.tensor_scalar(D_, D_, 257.0, None, ALU.add))
        V(lambda e: e.tensor_scalar(tmp, D_, 11, None, ALU.logical_shift_right))
        V(lambda e: e.tensor_copy(rec_hi[:, :], tmp))
        V(lambda e: e.tensor_scalar(D_, D_, 2047, None, ALU.bitwise_and))
        V(lambda e: e.tensor_copy(rec_lo[:, :], D_))
        V(lambda e: e.memset(starts[:, :, 0:1], 0.0))
        raw.close()
        hotr = sb(sort, "row_onehots", [PARTS, 2, PARTS, CHUNK], bf16)
        hotc = sb(sort, "col_onehots", [PARTS, PARTS, CHUNK], bf16)
        recc = sb(sort, "col_records", [PARTS, 2, 2, PARTS, CHUNK], f16)

        def spread(col, n, m):
            return col.rearrange("p (a m) -> p a m", a=1).to_broadcast([PARTS, n, m])

        hot_free = [None, None]
        hot_made = {}

        def hotv(g):
            return hot[:, g % 2, :].rearrange("p (c b t) -> p c b t", b=NB, t=HC)

        def make_hot(g):
            for c in range(-(-g_tiles[g] // HC)):
                m = min(HC, g_tiles[g] - c * HC)
                c0 = g * TPG + c * HC
                hot_made[g, c] = VE.put(lambda e, c=c, m=m, c0=c0: e.tensor_tensor(
                    hotv(g)[:, c, :, 0:m], spread(blk[:, c0:c0 + m], NB, m), rowbc[:, :, 0:m], ALU.is_equal),
                    some(hot_free[g % 2], rows, (ve, ve.value)), ve)

        def tile_hot(g, t):
            return hotv(g)[:, t // HC, :, t % HC]

        COUNT, BASE = bank[3], bank[4]
        counted = {}

        def count(g):
            for t in range(g_tiles[g]):
                counted[g] = PE.put(lambda e, t=t: e.matmul(
                    COUNT[0:TPG, 0:NB], pick[:, TPG - 1 - t:2 * TPG - 1 - t], tile_hot(g, t),
                    start=t == 0, stop=t == g_tiles[g] - 1), some(hot_made[g, t // HC], base_made.get(g - 1)), pe)

        base_made = {}

        def bases(g):
            a = V(lambda e: e.tensor_copy(cntb[0:TPG, :], COUNT[0:TPG, 0:NB]), counted[g])
            PE.put(lambda e: e.matmul(BASE[0:TPG, 0:NB], before[0:TPG, 0:TPG], cntb[0:TPG, :], start=True, stop=True), (a,), pe)
            b = PE.put(lambda e: e.matmul(BASE[:, NB:2 * NB], ones[0:TPG, :], cntb[0:TPG, :], start=True, stop=True), (a,), pe)
            V(lambda e: e.tensor_scalar(toti[:, :], BASE[:, NB:2 * NB], float(UNIT - 1), None, ALU.add), b)
            V(lambda e: e.tensor_scalar(toti[:, :], toti[:, :], 3, None, ALU.logical_shift_right))
            V(lambda e: e.tensor_copy(units[:, g, :], toti[:, :]))
            V(lambda e: e.tensor_tensor_scan(starts[:, g, 1:NB + 1], units[:, g, :], units[:, g, :], 0.0, ALU.add, ALU.bypass))
            V(lambda e: e.scalar_tensor_tensor(basei[0:TPG, 0, :], starts[0:TPG, g, 0:NB], float(UNIT), BASE[0:TPG, 0:NB], ALU.mult, ALU.add))
            V(lambda e: e.tensor_scalar(basei[0:TPG, 1, :], basei[0:TPG, 0, :], -PARTS, None, ALU.bitwise_and))
            V(lambda e: e.tensor_scalar(basei[0:TPG, 2, :], basei[0:TPG, 0, :], PARTS - 1, None, ALU.bitwise_and))
            base_made[g] = V(lambda e: e.tensor_copy(base[0:TPG, :, :], basei[0:TPG, 1:3, :]), *some(placed.get(g - 1)))

        PL = [bank[0], bank[1], bank[2]]
        pl_free = [None] * 3
        pl_n = [0]
        placed, pos_done, recc_free, hr_free = {}, {}, [None] * 2, [None] * 2

        def place(g):
            T = g_tiles[g]
            for t0 in range(0, T, PB):
                m = min(PB, T - t0)
                k = pl_n[0] % 3
                pl_n[0] += 1
                P = PL[k]
                for t in range(t0, t0 + m):
                    o = P[:, (t - t0) * NB:(t - t0 + 1) * NB]
                    sel = identb[0:TPG, t:t + 1].to_broadcast([TPG, PARTS])
                    PE.put(lambda e, o=o, sel=sel: e.matmul(o, sel, base[0:TPG, 0, :], start=True, stop=False),
                           some(base_made[g], pl_free[k]), pe)
                    PE.put(lambda e, o=o, sel=sel: e.matmul(o, sel, base[0:TPG, 1, :], start=False, stop=False), (), pe)
                    placed[g] = PE.put(lambda e, o=o, t=t: e.matmul(o, before_far[:, :], tile_hot(g, t), start=False, stop=True), (), pe)
                pl_free[k] = VE.put(lambda e, P=P, t0=t0, m=m: e.tensor_reduce(
                    pos[:, t0:t0 + m], P[:, 0:m * NB].rearrange("p (t b) -> p t b", b=NB), AX.X, ALU.max), (placed[g], (ve, pos_free[0])), ve)
            hot_free[g % 2] = placed[g]
            V(lambda e: e.tensor_scalar(posi[:, 0:T], pos[:, 0:T], -FAR, None, ALU.add))
            V(lambda e: e.tensor_scalar(prc[:, 0, 0:T], posi[:, 0:T], 7, None, ALU.arith_shift_right))
            V(lambda e: e.tensor_scalar(prc[:, 1, 0:T], posi[:, 0:T], PARTS - 1, None, ALU.bitwise_and))
            V(lambda e: e.tensor_scalar(prow[:, 0:T], prc[:, 0, 0:T], 1.0, None, ALU.add))
            pos_done[g] = V(lambda e: e.tensor_scalar(pcol[:, 0:T], prc[:, 1, 0:T], 1.0, None, ALU.add))
            pos_free[0] = ve.value

        pos_free = [0]
        OUTP = [bank[5], bank[6]]
        outp_free = [None] * 2
        sorted_done = {}
        n_chunk = [0]

        def scatter(g):
            T = g_tiles[g]
            O = OUTP[g % 2]
            for c in range(0, T, CHUNK):
                m = min(CHUNK, T - c)
                c0 = g * TPG + c
                k = n_chunk[0] % 2
                n_chunk[0] += 1
                VE.put(lambda e, c=c, m=m, k=k: e.tensor_tensor(hotr[:, k, :, 0:m], spread(prow[:, c:c + m], PARTS, m), row1c[:, :, 0:m], ALU.is_equal),
                       some(recc_free[k], pos_done[g]), ve)
                b = VE.put(lambda e, c=c, m=m: e.tensor_tensor(hotc[:, :, 0:m], spread(pcol[:, c:c + m], PARTS, m), row1c[:, :, 0:m], ALU.is_equal),
                           [(ve, ve.value - 1)], ve)
                for h, rec in enumerate((rec_hi, rec_lo)):
                    b2 = VE.put(lambda e, h=h, rec=rec, k=k, m=m, c0=c0: e.tensor_tensor(
                        recc[:, k, h, :, 0:m], hotc[:, :, 0:m], spread(rec[:, c0:c0 + m], PARTS, m), ALU.mult), (b,), ve)
                for t in range(m):
                    recc_free[k] = PE.put(lambda e, t=t, c=c, k=k: e.matmul(
                        O[:, 0:2 * PARTS], hotr[:, k, :, t], recc[:, k, :, :, t],
                        start=c + t == 0, stop=c + t == T - 1), some(b2, outp_free[g % 2]), pe)
            a = AC.put(lambda e: e.activation(shi[:, :], O[:, 0:PARTS], ACT.Copy, scale=2048.0),
                       some(recc_free[k], sorted_done.get(g - 1)), ac)
            finish[g] = a

        finish = {}

        def merge(g):
            O = OUTP[g % 2]
            outp_free[g % 2] = sorted_done[g] = VE.put(lambda e: e.tensor_tensor(
                sortd[:, g, :], shi[:, :], O[:, PARTS:2 * PARTS], ALU.add), (finish[g],), ve)

        make_hot(0)
        count(0)
        bases(0)
        for g in range(NG):
            if g + 1 < NG:
                make_hot(g + 1)
                count(g + 1)
            place(g)
            if g:
                merge(g - 1)
            if g + 1 < NG:
                bases(g + 1)
            scatter(g)
        merge(NG - 1)

        NE = NB + 1
        big = hot[:, :, :].rearrange("p a b -> p (a b)").bitcast(f32)
        half = UNITS_PER_ROW * NE
        at_least = [big[:, i * half:(i + 1) * half].rearrange("p (j b) -> p j b", b=NE) for i in range(2)]
        small = [big[:, 2 * half + i * NE:2 * half + (i + 1) * NE] for i in range(6)]
        assert 2 * half + 6 * NE + NG * NE <= big.shape[1]
        tot, pairs, pend, dcur, delta = (s_[:, 0:NB] for s_ in small[:5])
        toti2 = small[5][:, 0:NB].bitcast(i32)
        step = big[:, 2 * half + 6 * NE:2 * half + 6 * NE + NG * NE].rearrange("p (g b) -> p g b", b=NE)
        unit_no = sb(sort, "unit_number", [PARTS, UNITS_PER_ROW], f32)
        pair_no = sb(sort, "pair_number", [PARTS, MAPC], f32)
        bmf = sb(sort, "pair_block", [PARTS, MAPC], f32)
        PO.put(lambda e: e.iota(unit_no[:, :], [[1, UNITS_PER_ROW]], base=0, channel_multiplier=UNITS_PER_ROW,
                                allow_small_or_imprecise_dtypes=True), (), po)
        nos = PO.put(lambda e: e.iota(pair_no[:, :], [[1, MAPC]], base=0, channel_multiplier=MAPC,
                                      allow_small_or_imprecise_dtypes=True), (), po)
        V(lambda e: e.tensor_reduce(tot, units[:, :, :].rearrange("p g b -> p b g"), AX.X, ALU.add), (pe, pe.value))
        V(lambda e: e.tensor_scalar(toti2, tot, float(UNITS_PER_PAIR - 1), None, ALU.add))
        V(lambda e: e.tensor_scalar(toti2, toti2, 5, None, ALU.logical_shift_right))
        assert UNITS_PER_PAIR == 32
        V(lambda e: e.tensor_copy(pairs, toti2))
        V(lambda e: e.tensor_tensor_scan(pend, pairs, pairs, 0.0, ALU.add, ALU.bypass))
        V(lambda e: e.tensor_tensor(dcur, pend, pairs, ALU.subtract))
        V(lambda e: e.tensor_scalar(dcur, dcur, float(UNITS_PER_PAIR), None, ALU.mult))
        V(lambda e: e.memset(step[:, :, NB:NE], SKIP), nos)
        scat = sem("units_moved")
        for g in range(NG):
            V(lambda e, g=g: e.tensor_tensor(delta, dcur, starts[:, g, 0:NB], ALU.subtract))
            V(lambda e, g=g: e.tensor_tensor(dcur, dcur, units[:, g, :], ALU.add))
            V(lambda e, g=g: e.tensor_tensor(step[:, g, 1:NB], delta[:, 1:NB], delta[:, 0:NB - 1], ALU.subtract))
            V(lambda e, g=g: e.tensor_copy(step[:, g, 0:1], delta[:, 0:1]))
            V(lambda e, g=g: e.tensor_tensor(
                at_least[0], unit_no[:, :].rearrange("p (j a) -> p j a", a=1).to_broadcast([PARTS, UNITS_PER_ROW, NE]),
                spread(starts[:, g, :], UNITS_PER_ROW, NE), ALU.is_ge))
            V(lambda e, g=g: e.tensor_tensor(at_least[1], at_least[0], spread(step[:, g, :], UNITS_PER_ROW, NE), ALU.mult))
            V(lambda e, g=g: e.tensor_reduce(at_least[0][:, :, 0], at_least[1], AX.X, ALU.add))
            to = V(lambda e, g=g: e.tensor_tensor(dest[:, g * UNITS_PER_ROW:(g + 1) * UNITS_PER_ROW], at_least[0][:, :, 0],
                                                  unit_no[:, :], ALU.add))
            for j in range(UNITS_PER_ROW):
                PO.put(lambda e, g=g, j=j: e.indirect_dma_start(
                    slist, bass.IndirectOffsetOnAxis(ap=dest[:, g * UNITS_PER_ROW + j:g * UNITS_PER_ROW + j + 1].bitcast(u32), axis=0),
                    sortd[:, g, j * UNIT:(j + 1) * UNIT], None, bounds_check=LU - 1, oob_is_err=False), (to,), scat, 16)
        map_ge = big[:, 0:MAPC * NB].rearrange("p (j b) -> p j b", b=NB)
        V(lambda e: e.tensor_tensor(map_ge, pair_no[:, :].rearrange("p (j a) -> p j a", a=1).to_broadcast([PARTS, MAPC, NB]),
                                    spread(pend, MAPC, NB), ALU.is_ge))
        V(lambda e: e.tensor_reduce(bmf[:, :], map_ge, AX.X, ALU.add))
        V(lambda e: e.tensor_scalar(bmf[:, :], bmf[:, :], float(NB - 1), None, ALU.min))
        V(lambda e: e.tensor_scalar(bmap[:, 0, :], bmf[:, :], float(3 * A), None, ALU.mult))
        V(lambda e: e.tensor_scalar(bmap[:, 1, :], bmf[:, :], float(SUMS), None, ALU.mult))
        PO.put(None, [(scat, scat.value)])
        fence()
        sort.close()

        main = scope()
        sums = sb(main, "block_sums", [PARTS, NB * SUMS], f32)
        gidx = sb(main, "dst_rows", [PARTS, NTS], i32)
        lo = sb(main, "src_in_block", [PARTS, NTS], bf16)
        lof = sb(main, "src_in_block_f32", [PARTS, NTS], f32)
        score = sb(main, "scores", [PARTS, NTS], f32)
        RING = 6
        slot = sb(main, "gathered", [PARTS, RING, PAIR, SLOT], f32)
        oh = sb(main, "src_onehots", [PARTS, 2, PARTS, CHUNK], bf16)
        ohT = sb(main, "src_onehots_T", [PARTS, 3, PAIR * PARTS], bf16)
        ohw = sb(main, "weighted_onehots", [PARTS, 3, PAIR, PARTS], f32)
        ephi = sb(main, "e_times_phi", [PARTS, 2, PAIR, A], f32)
        wexp = sb(main, "edge_weight", [PARTS, 4, PAIR], f32)
        rows_sb = sums[:, 0:-(-NTS // PARTS) * PARTS]
        vi = score[:, :].bitcast(i32)
        NR = -(-NTS // PARTS)
        rw, rrest = NTS // PARTS, NTS % PARTS
        ll = sem("list_loaded")
        flat = slist.rearrange("(t a) u -> t (a u)", a=UNITS_PER_ROW)
        if rrest:
            z = VE.put(lambda e: e.memset(rows_sb[:, rw * PARTS:NR * PARTS], 0.0), (), ve)
            SP.put(lambda e: e.dma_start(rows_sb[0:rrest, rw * PARTS:NR * PARTS].bitcast(i32), flat[rw * PARTS:NTS, :]), (z,), ll, 16)
        if rw:
            SP.put(lambda e: e.dma_start(rows_sb[:, 0:rw * PARTS].rearrange("p (k e) -> p k e", e=PARTS).bitcast(i32),
                                         flat[0:rw * PARTS, :].rearrange("(k p) e -> p k e", p=PARTS)), (), ll, 16)
        V(lambda e: e.tensor_copy(rows_sb, rows_sb.bitcast(i32)), (ll, ll.value))
        LB = [bank[6], bank[7]]
        lb_free = [None] * 2
        for i in range(0, NR, 4):
            k = i // 4 % 2
            n = min(4, NR - i)
            for j in range(n):
                t = PE.put(lambda e, i=i, j=j, k=k: e.transpose(LB[k][:, j * PARTS:(j + 1) * PARTS],
                           rows_sb[:, (i + j) * PARTS:(i + j + 1) * PARTS], identf[:, :]), some(lb_free[k], (ve, ve.value)), pe)
            w = min(n * PARTS, NTS - i * PARTS)
            lb_free[k] = V(lambda e, i=i, k=k, w=w: e.tensor_copy(vi[:, i * PARTS:i * PARTS + w], LB[k][:, 0:w]), t)
        V(lambda e: e.tensor_scalar(gidx[:, :], vi, 8, None, ALU.logical_shift_right))
        V(lambda e: e.tensor_scalar(vi, vi, 255, None, ALU.bitwise_and))
        V(lambda e: e.tensor_copy(lof[:, :], vi))
        V(lambda e: e.tensor_copy(lo[:, :], vi))
        V(lambda e: e.memset(slot[:, :, :, SLOT - 1:SLOT], 1.0))
        SP.put(None, [(tab0, 16)])
        AC.put(None, [(tabx, 16)])
        fence()
        before_pass = {k: q.items for k, q in Q.items()}
        for q in Q.values():
            q.items, q.reached = [], {}

        mv, mp, ma, mg = sem("m_vector"), sem("m_tensor"), sem("m_scalar"), [sem(f"m_gathered_{i}") for i in range(RING)]
        mgp = sem("m_pool")
        QK, OT, SM = [bank[0], bank[1]], [bank[2], bank[3]], [bank[4], bank[5]]
        regs = {}
        H3 = NB * SUMS // 3
        z1 = VE.put(lambda e: e.memset(sums[:, 0:H3], 0.0), (), mv)
        z2 = PO.put(lambda e: e.memset(sums[:, H3:2 * H3], 0.0), (), mgp)
        z3 = VE.put(lambda e: e.memset(sums[:, 2 * H3:NB * SUMS], 0.0), (), mv)
        tok = {}

        def load_blocks(queue, name, which, c):
            p_, c_ = c * PAIRS_PER_CHUNK // MAPC, c * PAIRS_PER_CHUNK % MAPC

            def build(e):
                if name not in regs:
                    regs[name] = [e.alloc_register(f"{name}{i}") for i in range(PAIRS_PER_CHUNK)]
                return e.load(regs[name], bmap[p_:p_ + 1, which, c_:c_ + PAIRS_PER_CHUNK])
            queue.put(build)

        def gather(p):
            r = p % RING
            for j in range(PAIR):
                t = p * PAIR + j
                tok["gather", p] = PO.put(lambda e, t=t, j=j: e.indirect_dma_start(
                    slot[:, r, j, 0:ROW], None, table, bass.IndirectOffsetOnAxis(ap=gidx[:, t:t + 1].bitcast(u32), axis=0)),
                    some(tok.get(("sum", p - RING))), mg[r], 16)

        def onehots(c):
            k = c % 2
            tok["oh", c] = VE.put(lambda e: e.tensor_tensor(oh[:, k, :, :], spread(lo[:, c * CHUNK:(c + 1) * CHUNK], PARTS, CHUNK),
                                                            row1c[:, :, :], ALU.is_equal),
                                  some(tok.get(("turn", (c - 1) * PAIRS_PER_CHUNK - 1))), mv)

        def turn(p):
            c, k = p // PAIRS_PER_CHUNK, p // PAIRS_PER_CHUNK % 2
            O = OT[p % 2][:, 0:PARTS].bitcast(bf16)
            for j in range(PAIR):
                t = p * PAIR + j
                tok["turn", p] = PE.put(lambda e, t=t, j=j: e.transpose(O[:, j * PARTS:(j + 1) * PARTS], oh[:, k, :, t % CHUNK], identb[:, :]),
                                        some(tok["oh", c], tok.get(("ohT", p - 2))), mp)
            tok["ohT", p] = AC.put(lambda e: e.activation(ohT[:, p % 3, :], O, ACT.Copy), some(tok["turn", p], tok.get(("qk", p - 3))), ma)

        def qk(p):
            if p % PAIRS_PER_CHUNK == 0:
                load_blocks(PE, "pe_block", 0, p // PAIRS_PER_CHUNK)
            K, r = QK[p % 2], p % RING
            PE.put(lambda e: e.matmul(K[:, 0:PAIR * A], identf[:, :], slot[:, r, :, 0:A], start=True, stop=False),
                   some(tok["gather", p], tok.get(("e", p - 2))), mp)
            for j in range(PAIR):
                for s_ in range(3):
                    def build(e, j=j, s_=s_):
                        b = e.snap(regs["pe_block"][p % PAIRS_PER_CHUNK], min_val=0, max_val=(NB - 1) * 3 * A)
                        return e.matmul(K[:, j * A:(j + 1) * A], ohT[:, p % 3, j * PARTS:(j + 1) * PARTS],
                                        q3[:, bass.ds(b + s_ * A, A)], start=False, stop=s_ == 2 and j == PAIR - 1)
                    tok["qk", p] = PE.put(build, (tok["ohT", p],), mp)
            tok["e", p] = AC.put(lambda e: e.activation(slot[:, r, :, ROW:ROW + A], K[:, 0:PAIR * A].rearrange("p (j f) -> p j f", f=A), ACT.Tanh),
                                 (tok["qk", p],), ma)

        def scores(p):
            r, k = p % RING, p % 2
            a = VE.put(lambda e: e.tensor_tensor(ephi[:, k], slot[:, r, :, ROW:ROW + A], spread(phi[:, :], PAIR, A), ALU.mult),
                       some(tok["e", p], tok.get(("score", p - 2))), mv)
            tok["ephi", p] = a

        def scores2(p):
            k = p % 2
            tok["score", p] = VE.put(lambda e: e.tensor_reduce(score[:, p * PAIR:(p + 1) * PAIR], ephi[:, k], AX.X, ALU.add),
                                     (tok["ephi", p],), mv)
            tok["exp", p] = AC.put(lambda e: e.activation(wexp[:, p % 4, :], score[:, p * PAIR:(p + 1) * PAIR], ACT.Exp, bias=NSHIFT),
                                   some(tok["score", p], tok.get(("ohw", p - 4))), ma)

        def weigh(p):
            for j in range(PAIR):
                t = p * PAIR + j
                tok["ohw", p] = VE.put(lambda e, t=t, j=j: e.tensor_scalar(ohw[:, p % 3, j, :], row1[:, :], lof[:, t:t + 1], wexp[:, p % 4, j:j + 1],
                                                                          ALU.is_equal, ALU.mult),
                                       some(tok["exp", p], tok.get(("sum", p - 3))), mv)

        def total(p):
            M, r = SM[p % 2], p % RING
            for j in range(PAIR):
                tok["sum", p] = PE.put(lambda e, j=j: e.matmul(M[:, 0:SUMS], ohw[:, p % 3, j, :], slot[:, r, j, A:SLOT], start=j == 0, stop=j == PAIR - 1),
                                       some(tok["ohw", p], tok.get(("acc", p - 2))), mp)

        def accumulate(p):
            if p % PAIRS_PER_CHUNK == 0:
                load_blocks(VE, "ve_block", 1, p // PAIRS_PER_CHUNK)

            def build(e):
                b = e.snap(regs["ve_block"][p % PAIRS_PER_CHUNK], min_val=0, max_val=(NB - 1) * SUMS)
                return e.tensor_tensor(sums[:, bass.ds(b, SUMS)], sums[:, bass.ds(b, SUMS)], SM[p % 2][:, 0:SUMS], ALU.add)
            tok["acc", p] = VE.put(build, some(tok["sum", p], tok.get(("acc", p - 1)), z1, z2, z3), mv)

        STAGES = [(gather, 0), (turn, 1), (qk, 2), (scores, 3), (total, 5), (scores2, 3), (accumulate, 6), (weigh, 4)]
        for p in range(NP + 6):
            if p < NP and p % PAIRS_PER_CHUNK == 0:
                onehots(p // PAIRS_PER_CHUNK)
            for stage, lag in STAGES:
                if 0 <= p - lag < NP:
                    stage(p - lag)
        VE.put(lambda e: e.tensor_reduce(RMAX, score[:, :], AX.X, ALU.max), (tok["score", NP - 1],), mv)
        m1 = PO.put(lambda e: e.partition_all_reduce(GMAX, RMAX, PARTS, bass.bass_isa.ReduceOp.max), [(mv, mv.value)], mgp)
        AC.put(lambda e: e.activation(TMP, GMAX, ACT.Exp, bias=NSHIFT), (m1,), ma)
        VE.put(lambda e: e.tensor_scalar(EPS9, TMP, 1e-9, None, ALU.mult), [(ma, ma.value)], mv)
        VE.put(lambda e: e.tensor_scalar(NSHIFT, GMAX, -1.0, None, ALU.mult), [(mv, mv.value)], mv)
        gathers_landed = [(c, c.value) for c in mg]
        one_pass = {k: q.items for k, q in Q.items()}
        for q in Q.values():
            q.items, q.reached = [], {}
        arrive = {k: sem(f"pass_over_{k}") for k in Q if k != "sync"}
        leave = {k: sem(f"pass_next_{k}") for k in Q if k != "sync"}
        pass_sems = [mv, mp, ma, mgp, *mg]

        fin = scope()
        FB = 2
        fx = sb(fin, "x_again", [PARTS, 3, FB, D], f32)
        tT = sb(fin, "sums_T", [PARTS, 2, FB, 2, PARTS], f32)
        rden = sb(fin, "one_over_weight", [PARTS, NB], f32)
        hres = sb(fin, "residual", [PARTS, 2, FB, D], f32)
        bst = sb(fin, "bn_stats", [PARTS, 2, FB, 6], f32)
        mvar = sb(fin, "mean_var", [PARTS, 2, FB, 2], f32)
        sd = sb(fin, "deviation", [PARTS, 2, 2, FB], f32)
        fo = sb(fin, "out_rows", [PARTS, 2, FB, D], f32)
        sv = sums[:, :].rearrange("p (b s) -> p b s", s=SUMS)
        V(lambda e: e.tensor_scalar(rden[:, :], sv[:, :, SUMS - 1], EPS9, None, ALU.add))
        V(lambda e: e.reciprocal(rden[:, :], rden[:, :]))
        V(lambda e: e.memset(TMP, 1e-5))
        fl = [sem(f"x_again_loaded_{i}") for i in range(3)]
        fs = [sem(f"out_stored_{i}") for i in range(2)]
        TT, NUM = [bank[0], bank[1]], [bank[2], bank[3]]
        tt_free, num_free, fx_free = [None] * 2, [None] * 2, [None] * 3
        tT_free, stored = [None] * 2, [None] * 2
        T1, TE = D, A + 1
        for i in range(-(-NB // FB)):
            s, s3, b0 = i % 2, i % 3, i * FB
            n = min(FB, NB - b0)
            whole = n if b0 + n < NB or LAST == PARTS else n - 1
            got = None
            w_ = some(fx_free[s3])
            if whole < n:
                w_ = [VE.put(lambda e, s3=s3, w=whole: e.memset(fx[:, s3, w, :], 0.0), w_, ve)]
            if whole:
                got = SP.put(lambda e, s3=s3, w=whole, b0=b0: e.dma_start(
                    fx[:, s3, 0:w, :], x[b0 * PARTS:(b0 + w) * PARTS, :].rearrange("(b p) d -> p b d", p=PARTS)), w_, fl[s3], 16)
            if whole < n:
                got = SP.put(lambda e, s3=s3, w=whole: e.dma_start(fx[0:LAST, s3, w, :], x[(NB - 1) * PARTS:N, :]), w_, fl[s3], 16)
            for j in range(n):
                PE.put(lambda e, s=s, j=j, b=b0 + j: e.transpose(TT[s][:, j * 256:j * 256 + PARTS], sv[:, b, 0:D], identf[:, :]), some(tt_free[s]), pe)
                t = PE.put(lambda e, s=s, j=j, b=b0 + j: e.transpose(TT[s][0:TE, j * 256 + PARTS:(j + 1) * 256], sv[:, b, D:SUMS], identf[:, :]), (), pe)
            ttv = TT[s][:, 0:n * 256].rearrange("p (j a c) -> p j a c", a=2, c=PARTS)
            AC.put(lambda e, s=s, n=n, ttv=ttv: e.activation(tT[:, s, 0:n, 0, :], ttv[:, :, 0, :], ACT.Copy), some(t, tT_free[s]), ac)
            tt_free[s] = AC.put(lambda e, s=s, n=n, ttv=ttv: e.activation(tT[0:TE, s, 0:n, 1, :], ttv[0:TE, :, 1, :], ACT.Copy), (), ac)
            for j in range(n):
                o = NUM[s][:, j * D:(j + 1) * D]
                PE.put(lambda e, s=s, j=j, o=o: e.matmul(o, tT[:, s, j, 0, :], wy[:, :], start=True, stop=False), some(tt_free[s], num_free[s]), pe)
                t = PE.put(lambda e, s=s, j=j, o=o: e.matmul(o, tT[0:TE, s, j, 1, :], web[:, :], start=False, stop=True), (), pe)
            tT_free[s] = t
            for j in range(n):
                a = VE.put(lambda e, s=s, s3=s3, j=j, b=b0 + j: e.scalar_tensor_tensor(
                    hres[:, s, j, :], NUM[s][:, j * D:(j + 1) * D], rden[:, b:b + 1], fx[:, s3, j, :], ALU.mult, ALU.add),
                    some(t, got, (ve, ve.value)), ve)
            num_free[s] = fx_free[s3] = a
            for j in range(n):
                a = VE.put(lambda e, s=s, j=j: e.bn_stats(bst[:, s, j, :], hres[:, s, j, :]), (a,), ve)
            for j in range(n):
                a = VE.put(lambda e, s=s, j=j: e.bn_aggr(mvar[:, s, j, :], bst[:, s, j, :]), (a,), ve)
            c = AC.put(lambda e, s=s, n=n: e.activation(sd[:, s, 0, 0:n], mvar[:, s, 0:n, 1], ACT.Sqrt, bias=TMP), (a,), ac)
            a = VE.put(lambda e, s=s, n=n: e.reciprocal(sd[:, s, 1, 0:n], sd[:, s, 0, 0:n]), (c,), ve)
            for j in range(n):
                b_ = VE.put(lambda e, s=s, j=j: e.tensor_scalar(fo[:, s, j, :], hres[:, s, j, :], mvar[:, s, j, 0:1], sd[:, s, 1, j:j + 1],
                                                               ALU.subtract, ALU.mult), some(a, stored[s]), ve)
            if whole:
                stored[s] = SP.put(lambda e, s=s, w=whole, b0=b0: e.dma_start(
                    out[b0 * PARTS:(b0 + w) * PARTS, :].rearrange("(b p) d -> p b d", p=PARTS), fo[:, s, 0:w, :]), (b_,), fs[s], 16)
            if whole < n:
                stored[s] = SP.put(lambda e, s=s, w=whole: e.dma_start(out[(NB - 1) * PARTS:N, :], fo[0:LAST, s, w, :]), (b_,), fs[s], 16)
        SP.put(None, [(c, c.value) for c in fs])
        after_pass = {k: q.items for k, q in Q.items()}

        def play(name, engine):
            q = Queue()
            q.items = before_pass[name]
            q.run(engine)
            reg = engine.alloc_register(f"passes_{name}")
            engine.reg_load(reg, passes[0:1, 0:1])
            with engine.Fori(0, engine.snap(reg, min_val=1, max_val=2)):
                q.items = one_pass[name]
                q.run(engine)
                if name == "sync":
                    for c in arrive.values():
                        engine.wait_ge(c.sem, 1)
                    for c in (*arrive.values(), *pass_sems):
                        engine.sem_clear(c.sem)
                    for c in leave.values():
                        engine.sem_inc(c.sem, 1)
                else:
                    if name == "gpsimd":
                        for c, value in gathers_landed:
                            engine.wait_ge(c.sem, value)
                        engine.dma_reset()
                    engine.drain().then_inc(arrive[name].sem, 1)
                    engine.wait_ge(leave[name].sem, 1)
                    engine.sem_inc(leave[name].sem, -1)
            q.items = after_pass[name]
            q.run(engine)

        block = ctx.enter_context(nc.Block())

        @block.sync
        def _(e):
            play("sync", e)

        @block.gpsimd
        def _(e):
            play("gpsimd", e)

        @block.vector
        def _(e):
            play("vector", e)

        @block.scalar
        def _(e):
            play("scalar", e)

        @block.tensor
        def _(e):
            play("tensor", e)
        fin.close()
        main.close()


_INS = ["x", "src", "dst", "L0_gnn_Wq", "L0_gnn_Wk", "L0_gnn_Wphi", "L0_gnn_Wy_w", "L0_gnn_Wy_b", "L0_gnn_We"]


def kernel(**inputs):
    import numpy as np
    import concourse.bacc as bacc
    from concourse.bass_utils import run_bass_kernel_spmd

    nc = bacc.Bacc("TRN2", target_bir_lowering=False, num_devices=1)
    arrays, args = {}, []
    for name in _INS:
        a = np.ascontiguousarray(inputs[name])
        arrays[f"in_{name}"] = a
        args.append(nc.dram_tensor(f"in_{name}", a.shape, mybir.dt.from_np(a.dtype), kind="ExternalInput").ap())
    shape = arrays["in_x"].shape
    args.append(nc.dram_tensor("out", shape, mybir.dt.float32, kind="ExternalOutput").ap())
    gnn_program(nc, *args)
    r = run_bass_kernel_spmd(nc, [arrays], core_ids=[0])
    return r.results[0]["out"]
```

```python
import concourse.bass as bass
from concourse import mybir
from contextlib import ExitStack

PARTS = 128
COLS = 64
UNIT = 4
PAIR = 2
UNITS_PER_PAIR = PAIR * PARTS // UNIT
UNITS_PER_ROW = COLS // UNIT
UNITS_PER_TILE = PARTS // UNIT
CHUNK = 16
PAIRS_PER_CHUNK = CHUNK // PAIR
LOOSE_BOUND = 30.0
FAR = 65536.0
SKIP = float(1 << 21)


class Counter:

    def __init__(self, sem):
        self.sem, self.value = sem, 0

    def add(self, by):
        self.value += by
        return (self, self.value)


class Queue:

    def __init__(self):
        self.items, self.reached = [], {}

    def put(self, build, waits=(), done=None, by=1):
        need = []
        for counter, value in waits:
            if self.reached.get(counter, 0) < value:
                self.reached[counter] = value
                need.append((counter.sem, value))
        self.items.append((need, build, done.sem if done else None, by))
        return done.add(by) if done else None

    def run(self, engine):
        for need, build, sem, by in self.items:
            for s, value in need:
                engine.wait_ge(s, value)
            made = build(engine) if build else None
            if sem is not None:
                made.then_inc(sem, by)
        self.items = []


def gnn_program(nc, x, src, dst, Wq, Wk, Wphi, Wy_w, Wy_b, We, out):
    f32, i32, u32 = mybir.dt.float32, mybir.dt.int32, mybir.dt.uint32
    bf16, f16 = mybir.dt.bfloat16, mybir.dt.float16
    ALU, ACT, AX = mybir.AluOpType, mybir.ActivationFunctionType, mybir.AxisListType

    N, D = x.shape
    E = src.shape[0]
    A = Wq.shape[1]
    NB = -(-N // PARTS)
    LAST = N - (NB - 1) * PARTS
    NT = -(-E // PARTS)
    EW = E // PARTS
    EREST = E - EW * PARTS
    ROW = A + D
    SUMS = D + A + 1
    SLOT = ROW + A + 1

    TPG = min(NT, (PARTS * COLS - NB * (UNIT - 1)) // PARTS)
    NG = -(-NT // TPG)
    g_tiles = [min(TPG, NT - g * TPG) for g in range(NG)]
    max_units = (E + NG * NB * (UNIT - 1)) // UNIT
    max_pairs = (max_units + NB * (UNITS_PER_PAIR - 1)) // UNITS_PER_PAIR
    NP = -(-max_pairs // PAIRS_PER_CHUNK) * PAIRS_PER_CHUNK
    NTS = NP * PAIR
    LU = NTS * UNITS_PER_TILE
    MAPC = 16
    assert NP <= PARTS * MAPC and N + 1 < 1 << 14 and NB * (UNIT - 1) < PARTS * COLS // 2
    HC = 32
    PB = 512 // NB
    GB = 4

    table = nc.dram_tensor("table", (N + 1, ROW), f32).ap()
    slist = nc.dram_tensor("sorted_list", (LU, UNIT), i32).ap()

    ctx = ExitStack()
    with ctx:
        def scope():
            return ExitStack()

        def sb(where, name, shape, dt):
            return where.enter_context(nc.sbuf_tensor(name, shape, dt))

        def sem(name):
            return Counter(ctx.enter_context(nc.semaphore(name)))

        bank = [ctx.enter_context(nc.psum_tensor(f"bank{i}", [PARTS, 512], f32)) for i in range(8)]

        row1 = sb(ctx, "row_1_to_128", [PARTS, PARTS], f32)
        part = sb(ctx, "partition_number", [PARTS, 1], f32)
        row1c = sb(ctx, "row_1_to_128_chunk", [PARTS, PARTS, CHUNK], bf16)
        identf = sb(ctx, "identity_f32", [PARTS, PARTS], f32)
        identb = sb(ctx, "identity_bf16", [PARTS, PARTS], bf16)
        before = sb(ctx, "before", [PARTS, PARTS], bf16)
        before_far = sb(ctx, "before_far", [PARTS, PARTS], bf16)
        ones = sb(ctx, "ones", [PARTS, PARTS], bf16)
        onesf = sb(ctx, "ones_f32", [1, PARTS], f32)
        pick = sb(ctx, "pick", [PARTS, 2 * TPG], bf16)
        wkq = sb(ctx, "wk_wq", [D, 2 * A], f32)
        wy = sb(ctx, "wy", [D, D], f32)
        web = sb(ctx, "we_bias", [A + 1, D], f32)
        phi = sb(ctx, "phi", [PARTS, A], f32)
        row0 = sb(ctx, "table_row_0", [1, ROW], f32)
        stat = sb(ctx, "stat", [PARTS, 8], f32)
        BOUND, NSHIFT, RMAX, GMAX, EPS9, TMP = (stat[:, i:i + 1] for i in range(6))
        passes = sb(ctx, "passes", [1, 1], i32)
        used = sb(ctx, "pairs_used", [1, 1], i32)
        q3 = sb(ctx, "q_parts", [PARTS, NB * 3 * A], bf16)
        bmap = sb(ctx, "pair_blocks", [PARTS, 2, MAPC], i32)

        Q = {k: Queue() for k in ("sync", "gpsimd", "vector", "scalar", "tensor")}
        SP, PO, VE, AC, PE = (Q[k] for k in ("sync", "gpsimd", "vector", "scalar", "tensor"))
        po, ve, ac, pe = sem("pool_done"), sem("vector_done"), sem("scalar_done"), sem("tensor_done")
        fence_sems = {k: sem(f"fence_{k}") for k in Q}

        def V(build, *waits):
            return VE.put(build, [(ve, ve.value), *waits] if ve.value else waits, ve)

        def fence():
            for k, q in Q.items():
                q.put(lambda e: e.drain(), (), fence_sems[k])
            for k, q in Q.items():
                q.put(None, [(c, c.value) for j, c in fence_sems.items() if j != k])

        sort, early = scope(), scope()
        blk = sb(sort, "edge_block", [PARTS, NT], bf16)
        rec_hi = sb(sort, "record_high", [PARTS, NT], f16)
        rec_lo = sb(sort, "record_low", [PARTS, NT], f32)
        rowbc = sb(sort, "row_0_to_nb_chunk", [PARTS, NB, HC], bf16)
        sortd = sb(sort, "sorted_groups", [PARTS, NG, COLS], i32)
        dest = sb(sort, "unit_destinations", [PARTS, NG * UNITS_PER_ROW], i32)
        counts = sb(sort, "tile_block_counts", [PARTS, NG, NB], bf16)
        base = sb(sort, "base_parts", [PARTS, 2, NG, NB], bf16)
        units = sb(sort, "run_units", [PARTS, NG, NB], f16)
        starts = sb(sort, "run_starts", [PARTS, NG, NB + 1], f16)

        srcs = sb(early, "src_edges", [PARTS, NT], i32)
        dsts = sb(early, "dst_edges", [PARTS, NT], i32)
        HR = 3
        hot0 = sb(early, "block_onehots_to_count", [PARTS, HR, NB, HC], bf16)
        xin = sb(early, "x_in", [PARTS, 2, GB, D], f32)
        xT = sb(early, "xT", [PARTS, 2, GB * PARTS], f32)
        kst = sb(early, "k_and_q", [PARTS, 2, GB, 2 * A], f32)
        rest = sb(early, "q_rest", [PARTS, 2, GB, A], f32)
        ZU = max(z for z in range(1, 65) if LU // PARTS % z == 0)
        zeros = sb(early, "zero_units", [PARTS, ZU * UNIT], i32)
        some = lambda *w: [z for z in w if z is not None]
        el = sem("edges_loaded")
        MANY = 1 << 20
        pads = None
        if EREST:
            VE.put(lambda e: e.memset(srcs[:, EW:NT], MANY), (), ve)
            pads = VE.put(lambda e: e.memset(dsts[:, EW:NT], 0), (), ve)
        for t_, a_ in ((srcs, src), (dsts, dst)):
            SP.put(lambda e, t_=t_, a_=a_: e.dma_start(t_[:, 0:EW], a_[0:EW * PARTS].rearrange("(p c) -> p c", p=PARTS)), (), el, 16)
            if EREST:
                SP.put(lambda e, t_=t_, a_=a_: e.dma_start(t_[0:EREST, EW:NT], a_[EW * PARTS:E].rearrange("(p c) -> p c", c=1)), (pads,), el, 16)

        ld = sem("weights_loaded")
        for dst_ap, src_ap in ((wkq[:, 0:A], Wk), (wkq[:, A:2 * A], Wq), (wy[:, :], Wy_w),
                               (web[0:A, :], We), (web[A:A + 1, :], Wy_b.rearrange("(a n) -> a n", a=1)),
                               (phi[:, :], Wphi.rearrange("(a n) -> a n", a=1).to_broadcast([PARTS, A]))):
            loaded = SP.put(lambda e, d=dst_ap, s=src_ap: e.dma_start(d, s), (), ld, 16)
        tabx = sem("table_x_written")

        PO.put(lambda e: e.iota(row1[:, :], [[1, PARTS]], base=1, channel_multiplier=0,
                                allow_small_or_imprecise_dtypes=True), (), po)
        PO.put(lambda e: e.iota(part[:, :], [[0, 1]], base=1, channel_multiplier=1,
                                allow_small_or_imprecise_dtypes=True), (), po)
        iotas = PO.put(lambda e: e.iota(row1c[:, :, :], [[1, PARTS], [0, CHUNK]], base=1, channel_multiplier=0,
                                        allow_small_or_imprecise_dtypes=True), (), po)
        V(lambda e: e.tensor_scalar(identf[:, :], row1[:, :], part[:, :], None, ALU.is_equal), iotas)
        V(lambda e: e.tensor_scalar(identb[:, :], row1[:, :], part[:, :], None, ALU.is_equal))
        V(lambda e: e.tensor_scalar(before[:, :], row1[:, :], part[:, :], None, ALU.is_gt))
        V(lambda e: e.scalar_tensor_tensor(before_far[:, :], identf[:, :], FAR, before[:, :], ALU.mult, ALU.add))
        V(lambda e: e.memset(ones[:, :], 1.0))
        V(lambda e: e.memset(onesf[:, :], 1.0))
        V(lambda e: e.memset(pick[:, :], 0.0))
        V(lambda e: e.memset(pick[:, TPG - 1:TPG], 1.0))
        V(lambda e: e.tensor_reduce(BOUND, phi[:, :], AX.X, ALU.add, apply_absolute_value=True), loaded)
        V(lambda e: e.tensor_scalar(NSHIFT, BOUND, -1.0, None, ALU.mult))
        V(lambda e: e.tensor_scalar(passes[:, :], BOUND[0:1, :], LOOSE_BOUND, 1.0, ALU.is_ge, ALU.add))
        consts = (ve, ve.value)
        V(lambda e: e.memset(row0[:, :], 0.0))
        V(lambda e: e.tensor_scalar(row0[:, 0:A], phi[0:1, :], 0.0, 60.0, ALU.is_lt, ALU.mult))
        row0_made = V(lambda e: e.tensor_scalar(row0[:, 0:A], row0[:, 0:A], -30.0, None, ALU.add))
        tab0 = sem("table_row_0_written")
        SP.put(lambda e: e.dma_start(table[0:1, :], row0[:, :]), (row0_made,), tab0, 16)


        def spread(col, n, m):
            return col.rearrange("p (a m) -> p a m", a=1).to_broadcast([PARTS, n, m])

        zeroed = PO.put(lambda e: e.memset(zeros[:, :], 0), (), po)
        lz = sem("list_zeroed")

        def zero_list():
            AC.put(lambda e: e.dma_start(slist.rearrange("(p r a) u -> p r (a u)", p=PARTS, a=ZU), spread(zeros[:, :], LU // PARTS // ZU, ZU * UNIT)),
                   (zeroed,), lz, 16)

        TX = 4

        def table_x(i):
            r0, r1 = N * i // TX, N * (i + 1) // TX
            if r1 > r0:
                AC.put(lambda e: e.dma_start(table[1 + r0:1 + r1, A:ROW], x[r0:r1, :]), (), tabx, 16)

        rows = PO.put(lambda e: e.iota(rowbc[:, :, :], [[1, NB], [0, HC]], base=0, channel_multiplier=0,
                                       allow_small_or_imprecise_dtypes=True), (), po)
        S_ = srcs[:, :]
        D_ = dsts[:, :]
        tmp = sortd[:, :, :].rearrange("p g e -> p (g e)")[:, 0:NT]
        V(lambda e: e.tensor_scalar(tmp, S_, 7, None, ALU.logical_shift_right), (el, el.value))
        blk_made = V(lambda e: e.tensor_copy(blk[:, :], tmp))
        V(lambda e: e.tensor_scalar(S_, S_, PARTS - 1, None, ALU.bitwise_and))
        a = AC.put(lambda e: e.activation(D_, D_, ACT.Copy, scale=256.0, bias=257.0), some((el, el.value), pads), ac)
        V(lambda e: e.tensor_tensor(D_, D_, S_, ALU.add), a)
        a = V(lambda e: e.tensor_scalar(tmp, D_, 11, None, ALU.logical_shift_right))
        AC.put(lambda e: e.activation(rec_hi[:, :], tmp, ACT.Copy), (a,), ac)
        a = V(lambda e: e.tensor_scalar(D_, D_, 2047, None, ALU.bitwise_and))
        AC.put(lambda e: e.activation(rec_lo[:, :], D_, ACT.Copy), (a,), ac)
        V(lambda e: e.memset(starts[:, :, 0:1], 0.0))
        edges_split = blk_made[1]

        COUNT = [bank[4], bank[5]]
        count_free = [None] * 2
        hot0_n, hot0_free = [0], [None] * HR

        def count(g):
            C, T = COUNT[g % 2], g_tiles[g]
            for c0 in range(0, T, HC):
                k, m = hot0_n[0] % HR, min(HC, T - c0)
                hot0_n[0] += 1
                made = VE.put(lambda e, k=k, m=m, a=g * TPG + c0: e.tensor_tensor(
                    hot0[:, k, :, 0:m], spread(blk[:, a:a + m], NB, m), rowbc[:, :, 0:m], ALU.is_equal),
                    some(hot0_free[k], rows, (ve, edges_split)), ve)
                for t in range(c0, c0 + m):
                    hot0_free[k] = PE.put(lambda e, t=t, k=k, c0=c0: e.matmul(
                        C[0:TPG, 0:NB], pick[:, TPG - 1 - t:2 * TPG - 1 - t], hot0[:, k, :, t - c0],
                        start=t == 0, stop=t == T - 1), some(made, count_free[g % 2]), pe)
            count_free[g % 2] = AC.put(lambda e: e.activation(counts[0:TPG, g, :], C[0:TPG, 0:NB], ACT.Copy), (hot0_free[k],), ac)

        xl = [sem(f"x_loaded_{i}") for i in range(2)]
        ks = [sem(f"k_stored_{i}") for i in range(2)]
        q3v = q3[:, :].rearrange("p (b s f) -> p b s f", s=3, f=A)
        NQ = -(-NB // GB)
        n_ = {}

        def q_split(i):
            b0 = i * GB
            n = min(GB, NB - b0)
            return i % 2, b0, n, n if b0 + n < NB or LAST == PARTS else n - 1

        def node_load(i):
            s, b0, n, whole = q_split(i)
            waits = some(n_.get(("turn", i - 2)))
            if whole < n:
                waits = [VE.put(lambda e: e.memset(xin[:, s, whole, :], 0.0), waits, ve)]
            if whole:
                n_["load", i] = SP.put(lambda e: e.dma_start(
                    xin[:, s, 0:whole, :], x[b0 * PARTS:(b0 + whole) * PARTS, :].rearrange("(b p) d -> p b d", p=PARTS)),
                    waits, xl[s], 16)
            if whole < n:
                n_["load", i] = SP.put(lambda e: e.dma_start(xin[0:LAST, s, whole, :], x[(NB - 1) * PARTS:N, :]), waits, xl[s], 16)

        def node_turn(i):
            s, b0, n, whole = q_split(i)
            X = bank[s]
            for j in range(n):
                n_["turn", i] = PE.put(lambda e, j=j: e.transpose(X[:, j * PARTS:(j + 1) * PARTS], xin[:, s, j, :], identf[:, :]),
                                       some(n_["load", i], n_.get(("xT", i - 2)), consts), pe)
            n_["xT", i] = AC.put(lambda e: e.activation(xT[:, s, 0:n * PARTS], X[:, 0:n * PARTS], ACT.Copy),
                                 some(n_["turn", i], n_.get(("kq", i - 2))), ac)

        def node_product(i):
            s, b0, n, whole = q_split(i)
            B_ = bank[2 + s]
            for j in range(n):
                n_["kq", i] = PE.put(lambda e, j=j: e.matmul(B_[:, j * 2 * A:(j + 1) * 2 * A], xT[:, s, j * PARTS:(j + 1) * PARTS],
                                                             wkq[:, :], start=True, stop=True),
                                     some(n_["xT", i], n_.get(("kq_out", i - 2)), loaded), pe)
            kq = B_[:, 0:n * 2 * A].rearrange("p (b c) -> p b c", c=2 * A)
            n_["kq_out", i] = AC.put(lambda e: e.activation(kst[:, s, 0:n, :], kq, ACT.Copy),
                                     some(n_["kq", i], n_.get(("k_stored", i - 2)), n_.get(("q", i - 2))), ac)
            for w0, w, r in [(0, whole, PARTS)] * (whole > 0) + [(whole, 1, LAST)] * (whole < n):
                r0 = 1 + (b0 + w0) * PARTS
                n_["k_stored", i] = AC.put(lambda e, w0=w0, w=w, r=r, r0=r0: e.dma_start(
                    table[r0:r0 + (w - 1) * PARTS + r, 0:A].rearrange("(b p) f -> p b f", p=r),
                    kst[0:r, s, w0:w0 + w, 0:A]), (n_["kq_out", i],), ks[s], 16)

        def node_q0(i):
            s, b0, n, whole = q_split(i)
            n_["q0", i] = AC.put(lambda e: e.activation(q3v[:, b0:b0 + n, 0, :], kst[:, s, 0:n, A:2 * A], ACT.Copy), (n_["kq_out", i],), ac)

        def node_q1(i):
            s, b0, n, whole = q_split(i)
            n_["q", i] = VE.put(lambda e: e.tensor_tensor(rest[:, s, 0:n, :], kst[:, s, 0:n, A:2 * A], q3v[:, b0:b0 + n, 0, :], ALU.subtract),
                                some(n_["q0", i], n_.get(("q2", i - 2))), ve)
            n_["q1", i] = AC.put(lambda e: e.activation(q3v[:, b0:b0 + n, 1, :], rest[:, s, 0:n, :], ACT.Copy), (n_["q", i],), ac)

        def node_q2(i):
            s, b0, n, whole = q_split(i)
            n_["q2", i] = VE.put(lambda e: e.tensor_tensor(q3v[:, b0:b0 + n, 2, :], rest[:, s, 0:n, :], q3v[:, b0:b0 + n, 1, :], ALU.subtract),
                                 (n_["q1", i],), ve)

        N_STAGES = [(node_load, 0), (node_turn, 1), (node_product, 2), (node_q0, 2), (node_q1, 3), (node_q2, 4)]
        for i in range(max(NG, NQ + 4)):
            for stage, lag in N_STAGES:
                if 0 <= i - lag < NQ:
                    stage(i - lag)
            if i < NG:
                count(i)
            if 1 <= i <= TX:
                table_x(i - 1)
            if i == 0:
                zero_list()
        for i in range(max(NG, NQ + 4), TX + 1):
            table_x(i - 1)

        SP.put(None, [(c, c.value) for c in (*xl, *ks)])
        AC.put(None, [(lz, 16)])
        fence()
        early.close()

        NE = NB + 1
        UPG = PARTS * UNITS_PER_ROW
        plan = scope()
        basei = sb(plan, "base_int", [PARTS, 3, PB, NB], i32)
        toti = basei[:, 0, :, :]
        unit_row = sb(plan, "unit_number_row", [PARTS, UPG], f16)
        unit_no = sb(plan, "unit_number", [PARTS, UNITS_PER_ROW], f32)
        ge = sb(plan, "unit_at_or_past_start", [PARTS, 2, UPG], f16)
        map_ge = sb(plan, "pair_past_block", [PARTS, MAPC, NB], bf16)
        stepi = sb(plan, "steps_int", [PARTS, 3, NG], i32)
        steph = sb(plan, "step_parts", [PARTS, NG, 2], f16)
        destf = sb(plan, "unit_destinations_f32", [PARTS, NG * UNITS_PER_ROW], f32)
        pair_no = sb(plan, "pair_number", [PARTS, MAPC], f32)
        bmf = sb(plan, "pair_block", [PARTS, MAPC], f32)
        minus = sb(plan, "minus_the_one_before", [PARTS, PARTS], f32)
        rowp = sb(plan, "row_block_pairs", [PARTS, 3, NB], f32)
        colf = sb(plan, "col_starts_units", [PARTS, 6, NG], f32)
        colp = sb(plan, "col_block_pairs", [PARTS, 4], f32)
        colpi = sb(plan, "col_block_pairs_int", [PARTS, 1], i32)
        colph = sb(plan, "col_block_pairs_f16", [PARTS, 1], f16)
        PO.put(lambda e: e.iota(unit_row[:, :], [[1, UPG]], base=0, channel_multiplier=0,
                                allow_small_or_imprecise_dtypes=True), (), po)
        PO.put(lambda e: e.iota(unit_no[:, :], [[1, UNITS_PER_ROW]], base=0, channel_multiplier=UNITS_PER_ROW,
                                allow_small_or_imprecise_dtypes=True), (), po)
        UNIT_BITS, UPP_BITS = UNIT.bit_length() - 1, UNITS_PER_PAIR.bit_length() - 1
        nos = PO.put(lambda e: e.iota(pair_no[:, :], [[1, MAPC]], base=0, channel_multiplier=MAPC,
                                      allow_small_or_imprecise_dtypes=True), (), po)
        assert UNIT == 1 << UNIT_BITS and UNITS_PER_PAIR == 1 << UPP_BITS
        TOT, BASE = bank[6], bank[7]
        tot_free = base_free = None
        counted = (ac, ac.value)
        for g0 in range(0, NG, PB):
            m = min(PB, NG - g0)
            flat_c = counts[0:TPG, g0:g0 + m, :].rearrange("p g b -> p (g b)")
            v3 = lambda ap, m=m: ap[:, 0:m * NB].rearrange("p (g b) -> p g b", b=NB)
            a = PE.put(lambda e, f=flat_c, m=m: e.matmul(TOT[:, 0:m * NB], ones[0:TPG, :], f, start=True, stop=True), some(counted, tot_free), pe)
            b = PE.put(lambda e, f=flat_c, m=m: e.matmul(BASE[0:TPG, 0:m * NB], before[0:TPG, 0:TPG], f, start=True, stop=True), some(base_free), pe)
            tot_free = V(lambda e, m=m, v3=v3: e.tensor_scalar(toti[:, 0:m, :], v3(TOT[:, :]), float(UNIT - 1), None, ALU.add), a)
            V(lambda e, m=m: e.tensor_scalar(toti[:, 0:m, :], toti[:, 0:m, :], UNIT_BITS, None, ALU.logical_shift_right))
            V(lambda e, m=m, g0=g0: e.tensor_copy(units[:, g0:g0 + m, :], toti[:, 0:m, :]))
            unit_made = ve.value
            for g in range(g0, g0 + m):
                VE.put(lambda e, g=g: e.tensor_tensor_scan(starts[:, g, 1:NE], units[:, g, :], units[:, g, :], 0.0, ALU.add, ALU.bypass),
                       [(ve, unit_made)], ve)
            base_free = V(lambda e, m=m, g0=g0, v3=v3: e.scalar_tensor_tensor(
                basei[0:TPG, 0, 0:m, :], starts[0:TPG, g0:g0 + m, 0:NB], float(UNIT), v3(BASE[0:TPG, :]), ALU.mult, ALU.add), b)
            V(lambda e, m=m: e.tensor_scalar(basei[0:TPG, 1, 0:m, :], basei[0:TPG, 0, 0:m, :], -PARTS, None, ALU.bitwise_and))
            V(lambda e, m=m: e.tensor_scalar(basei[0:TPG, 2, 0:m, :], basei[0:TPG, 0, 0:m, :], PARTS - 1, None, ALU.bitwise_and))
            V(lambda e, m=m, g0=g0: e.tensor_copy(base[0:TPG, :, g0:g0 + m, :], basei[0:TPG, 1:3, 0:m, :]))
        COLB = bank[4]
        for g in range(NG):
            PE.put(lambda e, g=g: e.matmul(COLB[0:NE, g:g + 1], starts[0:1, g, :], ones[0:1, 0:1], start=True, stop=True), [(ve, ve.value)], pe)
            a = PE.put(lambda e, g=g: e.matmul(COLB[0:NB, NG + g:NG + g + 1], units[0:1, g, :], ones[0:1, 0:1], start=True, stop=True), (), pe)
        cstart, cunit, cupto, cdelta, cstep = (colf[:, i, :] for i in range(5))
        V(lambda e: e.tensor_copy(cstart[0:NE], COLB[0:NE, 0:NG]), a)
        V(lambda e: e.tensor_copy(cunit[0:NB], COLB[0:NB, NG:2 * NG]))
        V(lambda e: e.tensor_tensor_scan(cupto[0:NB], cunit[0:NB], cunit[0:NB], 0.0, ALU.add, ALU.bypass))
        V(lambda e: e.tensor_scalar(colpi[0:NB, :], cupto[0:NB, NG - 1:NG], float(UNITS_PER_PAIR - 1), None, ALU.add))
        V(lambda e: e.tensor_scalar(colpi[0:NB, :], colpi[0:NB, :], UPP_BITS, None, ALU.logical_shift_right))
        a = V(lambda e: e.tensor_copy(colph[0:NB, :], colpi[0:NB, :]))
        a = PE.put(lambda e: e.matmul(BASE[0:NB, 0:1], before[0:NB, 0:NB], colph[0:NB, :], start=True, stop=True), (a, base_free), pe)
        V(lambda e: e.tensor_scalar(colp[0:NB, 0:1], BASE[0:NB, 0:1], float(UNITS_PER_PAIR), None, ALU.mult), a)
        V(lambda e: e.tensor_tensor(cdelta[0:NB], cupto[0:NB], cunit[0:NB], ALU.subtract))
        V(lambda e: e.tensor_tensor(cdelta[0:NB], cdelta[0:NB], cstart[0:NB], ALU.subtract))
        V(lambda e: e.tensor_scalar(cdelta[0:NB], cdelta[0:NB], colp[0:NB, 0:1], None, ALU.add))
        V(lambda e: e.tensor_scalar(minus[:, :], row1[:, :], -1.0, part[:, :], ALU.add, ALU.is_equal))
        a = V(lambda e: e.tensor_tensor(minus[:, :], identf[:, :], minus[:, :], ALU.subtract))
        a = PE.put(lambda e: e.matmul(TOT[0:NE, 0:NG], minus[0:NB, 0:NE], cdelta[0:NB], start=True, stop=True), (a, tot_free), pe)
        V(lambda e: e.tensor_scalar(colp[:, 1:2], part[:, :], float(NE), SKIP, ALU.is_equal, ALU.mult))
        V(lambda e: e.tensor_scalar(cstep[0:NE], TOT[0:NE, 0:NG], colp[0:NE, 1:2], None, ALU.add), a)
        V(lambda e: e.tensor_copy(stepi[0:NE, 0, :], cstep[0:NE]))
        V(lambda e: e.tensor_scalar(stepi[0:NE, 1, :], stepi[0:NE, 0, :], 2047, None, ALU.bitwise_and))
        V(lambda e: e.tensor_scalar(stepi[0:NE, 2, :], stepi[0:NE, 0, :], 11, None, ALU.arith_shift_right))
        V(lambda e: e.tensor_copy(steph[0:NE, :, :].rearrange("p g s -> p s g"), stepi[0:NE, 1:3, :]))
        step_made = ve.value
        GH = 512 // (2 * UNITS_PER_ROW)
        DEST = bank[0:4]
        assert NG <= 4 * GH and UPG <= 2048
        ge_free = [None] * 2
        for g in range(NG):
            k = g % 2
            a = VE.put(lambda e, g=g, k=k: e.tensor_scalar(ge[0:NE, k, :], unit_row[0:NE, :], cstart[0:NE, g:g + 1], None, ALU.is_ge),
                       some(ge_free[k], nos, (ve, step_made)), ve)
            gv = ge[0:NE, k, :].rearrange("b (p j) -> b p j", j=UNITS_PER_ROW)
            for j in range(UNITS_PER_ROW):
                o = 2 * (g % GH * UNITS_PER_ROW + j)
                ge_free[k] = PE.put(lambda e, g=g, j=j, o=o, gv=gv: e.matmul(
                    DEST[g // GH][:, o:o + 2], gv[:, :, j], steph[0:NE, g, :], start=True, stop=True), (a,), pe)
        for h in range(-(-NG // GH)):
            m = min(GH, NG - h * GH)
            dv = DEST[h][:, 0:m * UNITS_PER_ROW * 2].rearrange("p (g j s) -> p g j s", g=m, s=2)
            df = destf[:, h * GH * UNITS_PER_ROW:(h * GH + m) * UNITS_PER_ROW].rearrange("p (g j) -> p g j", g=m)
            di = dest[:, h * GH * UNITS_PER_ROW:(h * GH + m) * UNITS_PER_ROW].rearrange("p (g j) -> p g j", g=m)
            V(lambda e, dv=dv, df=df, m=m: e.scalar_tensor_tensor(df, dv[:, :, :, 1], 2048.0, spread(unit_no[:, :], m, UNITS_PER_ROW), ALU.mult, ALU.add),
              *some(*ge_free))
            V(lambda e, dv=dv, df=df, di=di: e.tensor_tensor(di, df, dv[:, :, :, 0], ALU.add))
        tot, pairs, pend = (rowp[:, i, :] for i in range(3))
        toti2 = toti[:, 0, :]
        V(lambda e: e.tensor_reduce(tot, units[:, :, :].rearrange("p g b -> p b g"), AX.X, ALU.add))
        V(lambda e: e.tensor_scalar(toti2, tot, float(UNITS_PER_PAIR - 1), None, ALU.add))
        V(lambda e: e.tensor_scalar(toti2, toti2, UPP_BITS, None, ALU.logical_shift_right))
        V(lambda e: e.tensor_copy(pairs, toti2))
        V(lambda e: e.tensor_tensor_scan(pend, pairs, pairs, 0.0, ALU.add, ALU.bypass))
        V(lambda e: e.tensor_copy(used[:, :], pend[0:1, NB - 1:NB]))
        V(lambda e: e.tensor_tensor(map_ge[:, :, :], pair_no[:, :].rearrange("p (j a) -> p j a", a=1).to_broadcast([PARTS, MAPC, NB]),
                                    spread(pend, MAPC, NB), ALU.is_ge), nos)
        V(lambda e: e.tensor_reduce(bmf[:, :], map_ge[:, :, :], AX.X, ALU.add))
        V(lambda e: e.tensor_scalar(bmf[:, :], bmf[:, :], float(NB - 1), None, ALU.min))
        V(lambda e: e.tensor_scalar(bmap[:, 0, :], bmf[:, :], float(3 * A), None, ALU.mult))
        V(lambda e: e.tensor_scalar(bmap[:, 1, :], bmf[:, :], float(SUMS), None, ALU.mult))
        fence()
        plan.close()

        late = scope()
        NHC = -(-TPG // CHUNK)
        hot = sb(late, "block_onehots", [PARTS, 2, NHC, NB, CHUNK], bf16)
        hotr = sb(late, "row_onehots", [PARTS, 2, PARTS, CHUNK], bf16)
        hotc = sb(late, "col_onehots", [PARTS, 2, COLS, CHUNK], bf16)
        recc = sb(late, "col_records", [PARTS, 2, 2, COLS, CHUNK], f16)
        pos = sb(late, "places", [PARTS, 2, TPG], f32)
        posi = sb(late, "places_int", [PARTS, TPG], i32)
        prc = sb(late, "place_row_col_int", [PARTS, 2, TPG], i32)
        prow = sb(late, "place_row", [PARTS, 2, TPG], bf16)
        pcol = sb(late, "place_col", [PARTS, 2, TPG], bf16)
        shi = sb(late, "record_high_out", [PARTS, COLS], f32)
        relu = sb(late, "relu_out", [PARTS, 4, NB], bf16)
        near = sb(late, "one_minus_far", [PARTS, 1], f32)
        bias_of = sb(late, "place_bias", [PARTS, TPG], f32)

        def scalar_has(g, c, t0):
            return t0 == c * CHUNK and c < NHC - 1

        V(lambda e: e.memset(bias_of[:, :], -FAR))
        for c in range(NHC - 1):
            V(lambda e, t0=c * CHUNK: e.memset(bias_of[:, t0:t0 + min(PB, CHUNK)], -1.0))
        near_made = V(lambda e: e.memset(near[:, :], 1.0 - FAR))
        relu_n, relu_done, summed = [0], [None] * 4, {}
        hot_made, hot_free = {}, {}

        def make_hot(g, c):
            m = min(CHUNK, g_tiles[g] - c * CHUNK)
            a = g * TPG + c * CHUNK
            hot_made[g, c] = VE.put(lambda e: e.tensor_tensor(
                hot[:, g % 2, c, :, 0:m], spread(blk[:, a:a + m], NB, m), rowbc[:, :, 0:m], ALU.is_equal),
                some(hot_free.get((g - 2, c))), ve)

        PL = {VE: [bank[0], bank[1], bank[2], bank[7]], AC: [bank[3], bank[4]]}
        pl_free = {VE: [None] * 4, AC: [None] * 2}
        pl_n = {VE: 0, AC: 0}
        split_done, prow_free = {}, {}

        def place(g, c):
            T = min(g_tiles[g], (c + 1) * CHUNK)
            for t0 in range(c * CHUNK, T, PB):
                m = min(PB, T - t0)
                E_ = AC if scalar_has(g, c, t0) else VE
                k = pl_n[E_] % len(PL[E_])
                pl_n[E_] += 1
                P = PL[E_][k]
                for t in range(t0, t0 + m):
                    o = P[:, (t - t0) * NB:(t - t0 + 1) * NB]
                    sel = identb[0:TPG, t:t + 1].to_broadcast([TPG, PARTS])
                    PE.put(lambda e, o=o, sel=sel: e.matmul(o, sel, base[0:TPG, 0, g, :], start=True, stop=False),
                           some(pl_free[E_][k]), pe)
                    PE.put(lambda e, o=o, sel=sel: e.matmul(o, sel, base[0:TPG, 1, g, :], start=False, stop=False), (), pe)
                    placed = PE.put(lambda e, o=o, t=t: e.matmul(o, before_far[:, :], hot[:, g % 2, c, :, t - c * CHUNK], start=False, stop=True),
                                    (hot_made[g, c],), pe)
                if E_ is AC:
                    for t in range(t0, t0 + m):
                        w = relu_n[0] % len(relu_done)
                        relu_n[0] += 1
                        pl_free[AC][k] = relu_done[w] = AC.put(lambda e, P=P, t=t, t0=t0, w=w: e.activation(
                            relu[:, w, :], P[:, (t - t0) * NB:(t - t0 + 1) * NB], ACT.Relu, bias=near[:, :], accum_out=pos[:, g % 2, t:t + 1]),
                            some(placed, split_done.get(g - 2), relu_done[w], near_made), ac)
                    summed[g] = pl_free[AC][k]
                    continue
                pl_free[VE][k] = VE.put(lambda e, P=P, t0=t0, m=m: e.tensor_reduce(
                    pos[:, g % 2, t0:t0 + m], P[:, 0:m * NB].rearrange("p (t b) -> p t b", b=NB), AX.X, ALU.max),
                    some(placed, split_done.get(g - 2)), ve)
            hot_free[g, c] = placed

        def split_places(g):
            T = g_tiles[g]
            V(lambda e: e.tensor_tensor(posi[:, 0:T], pos[:, g % 2, 0:T], bias_of[:, 0:T], ALU.add), *some(summed.get(g)))
            V(lambda e: e.tensor_scalar(prc[:, 0, 0:T], posi[:, 0:T], COLS.bit_length() - 1, None, ALU.arith_shift_right))
            V(lambda e: e.tensor_scalar(prc[:, 1, 0:T], posi[:, 0:T], COLS - 1, None, ALU.bitwise_and))
            V(lambda e: e.tensor_scalar(prow[:, g % 2, 0:T], prc[:, 0, 0:T], 1.0, None, ALU.add))
            split_done[g] = V(lambda e: e.tensor_scalar(pcol[:, g % 2, 0:T], prc[:, 1, 0:T], 1.0, None, ALU.add))

        OUTP = [bank[5], bank[6]]
        outp_free = [None] * 2
        n_chunk = [0]
        rec_free, rec_made, gather_hi = [None] * 2, {}, {}
        move = sem("units_moved")

        def make_records(g, c):
            m = min(CHUNK, g_tiles[g] - c * CHUNK)
            a = g * TPG + c * CHUNK
            cols = slice(c * CHUNK, c * CHUNK + m)
            k = n_chunk[0] % 2
            n_chunk[0] += 1
            b = VE.put(lambda e: e.tensor_tensor(hotc[:, k, :, 0:m], spread(pcol[:, g % 2, cols], COLS, m), row1c[:, 0:COLS, 0:m], ALU.is_equal),
                       some(rec_free[k], split_done[g]), ve)
            VE.put(lambda e: e.tensor_tensor(hotr[:, k, :, 0:m], spread(prow[:, g % 2, cols], PARTS, m), row1c[:, :, 0:m], ALU.is_equal), (), ve)
            hi = VE.put(lambda e: e.tensor_tensor(recc[:, k, 0, :, 0:m], hotc[:, k, :, 0:m], spread(rec_hi[:, a:a + m], COLS, m), ALU.mult), (b,), ve)
            for t in range(m):
                rec_made[g, c] = AC.put(lambda e, t=t: e.activation(recc[:, k, 1, :, t], hotc[:, k, :, t], ACT.Copy, scale=rec_lo[:, a + t:a + t + 1]),
                             some(b, rec_free[k]), ac)
            rec_made[g, c] = (rec_made[g, c], hi, k)

        def add_records(g, c):
            T = g_tiles[g]
            O = OUTP[g % 2]
            lo_, hi, k = rec_made[g, c]
            for t in range(min(CHUNK, T - c * CHUNK)):
                last = PE.put(lambda e, t=t: e.matmul(O[:, 0:2 * COLS], hotr[:, k, :, t], recc[:, k, :, :, t],
                                                      start=c + t == 0, stop=c * CHUNK + t == T - 1), some(hi, lo_, outp_free[g % 2]), pe)
            rec_free[k] = last
            if c == -(-T // CHUNK) - 1:
                gather_hi[g] = AC.put(lambda e: e.activation(shi[:, :], O[:, 0:COLS], ACT.Copy, scale=2048.0),
                                      some(last, outp_free[(g - 1) % 2]), ac)

        def merge_and_move(g):
            O = OUTP[g % 2]
            done = outp_free[g % 2] = VE.put(lambda e: e.tensor_tensor(sortd[:, g, :], shi[:, :], O[:, COLS:2 * COLS], ALU.add), (gather_hi[g],), ve)
            for j in range(UNITS_PER_ROW):
                o = g * UNITS_PER_ROW + j
                PO.put(lambda e, j=j, o=o: e.indirect_dma_start(
                    slist, bass.IndirectOffsetOnAxis(ap=dest[:, o:o + 1].bitcast(u32), axis=0),
                    sortd[:, g, j * UNIT:(j + 1) * UNIT], None, bounds_check=LU - 1, oob_is_err=False), (done,), move, 16)

        owed = []

        def pay():
            for g_, c_ in owed:
                add_records(g_, c_)
                if (c_ + 1) * CHUNK >= g_tiles[g_]:
                    whole_groups.append(g_)
            owed.clear()

        whole_groups = []
        for g in range(-1, NG + 1):
            for c in range(NHC):
                made = 0 <= g - 1 and c * CHUNK < g_tiles[g - 1]
                if made:
                    make_records(g - 1, c)
                if 0 <= g < NG and c * CHUNK < g_tiles[g]:
                    place(g, c)
                if g + 1 < NG and c * CHUNK < g_tiles[g + 1]:
                    make_hot(g + 1, c)
                for w in whole_groups:
                    merge_and_move(w)
                whole_groups.clear()
                if made:
                    pay()
                    owed.append((g - 1, c))
            if 0 <= g < NG:
                split_places(g)
        pay()
        merge_and_move(NG - 1)
        PO.put(None, [(move, move.value)])
        fence()
        late.close()
        sort.close()

        main = scope()
        sums = sb(main, "block_sums", [PARTS, NB * SUMS], f32)
        lists = scope()
        gidx = sb(lists, "dst_rows", [PARTS, NTS], i32)
        lo = sb(lists, "src_in_block", [PARTS, NTS], bf16)
        lof = sb(lists, "src_in_block_f32", [PARTS, NTS], f32)
        score = sb(lists, "scores", [PARTS, NTS], f32)
        RING = 6
        slot = sb(lists, "gathered", [PARTS, RING, PAIR, SLOT], f32)
        oh = sb(lists, "src_onehots", [PARTS, 2, PARTS, CHUNK], bf16)
        ohT = sb(lists, "src_onehots_T", [PARTS, 3, PAIR * PARTS], bf16)
        ohw = sb(lists, "weighted_onehots", [PARTS, 3, PAIR, PARTS], f32)
        ephi = sb(lists, "e_times_phi", [PARTS, 2, PAIR, A], f32)
        wexp = sb(lists, "edge_weight", [PARTS, 4, PAIR], f32)
        rows_sb = sums[:, 0:-(-NTS // PARTS) * PARTS]
        vi = score[:, :].bitcast(i32)
        NR = -(-NTS // PARTS)
        rw, rrest = NTS // PARTS, NTS % PARTS
        ll = sem("list_loaded")
        flat = slist.rearrange("(t a) u -> t (a u)", a=UNITS_PER_TILE)
        if rrest:
            z = VE.put(lambda e: e.memset(rows_sb[:, rw * PARTS:NR * PARTS], 0.0), (), ve)
            SP.put(lambda e: e.dma_start(rows_sb[0:rrest, rw * PARTS:NR * PARTS].bitcast(i32), flat[rw * PARTS:NTS, :]), (z,), ll, 16)
        if rw:
            SP.put(lambda e: e.dma_start(rows_sb[:, 0:rw * PARTS].rearrange("p (k e) -> p k e", e=PARTS).bitcast(i32),
                                         flat[0:rw * PARTS, :].rearrange("(k p) e -> p k e", p=PARTS)), (), ll, 16)
        V(lambda e: e.tensor_copy(rows_sb, rows_sb.bitcast(i32)), (ll, ll.value))
        LB = [bank[6], bank[7]]
        lb_free = [None] * 2
        for i in range(0, NR, 4):
            k = i // 4 % 2
            n = min(4, NR - i)
            for j in range(n):
                t = PE.put(lambda e, i=i, j=j, k=k: e.transpose(LB[k][:, j * PARTS:(j + 1) * PARTS],
                           rows_sb[:, (i + j) * PARTS:(i + j + 1) * PARTS], identf[:, :]), some(lb_free[k], (ve, ve.value)), pe)
            w = min(n * PARTS, NTS - i * PARTS)
            lb_free[k] = V(lambda e, i=i, k=k, w=w: e.tensor_copy(vi[:, i * PARTS:i * PARTS + w], LB[k][:, 0:w]), t)
        V(lambda e: e.tensor_scalar(gidx[:, :], vi, 8, None, ALU.logical_shift_right))
        V(lambda e: e.tensor_scalar(vi, vi, 255, None, ALU.bitwise_and))
        V(lambda e: e.tensor_copy(lof[:, :], vi))
        V(lambda e: e.tensor_copy(lo[:, :], vi))
        V(lambda e: e.memset(slot[:, :, :, SLOT - 1:SLOT], 1.0))
        SP.put(None, [(tab0, 16)])
        AC.put(None, [(tabx, tabx.value)])
        fence()
        before_pass = {k: q.items for k, q in Q.items()}
        for q in Q.values():
            q.items, q.reached = [], {}

        mv, mp, ma, mg = sem("m_vector"), sem("m_tensor"), sem("m_scalar"), [sem(f"m_gathered_{i}") for i in range(RING)]
        mgp = sem("m_pool")
        QK, OT, SM = [bank[0], bank[1]], [bank[2], bank[3]], [bank[4], bank[5]]
        regs = {}
        H3 = NB * SUMS // 3
        z1 = VE.put(lambda e: e.memset(sums[:, 0:H3], 0.0), (), mv)
        z2 = PO.put(lambda e: e.memset(sums[:, H3:2 * H3], 0.0), (), mgp)
        z3 = VE.put(lambda e: e.memset(sums[:, 2 * H3:NB * SUMS], 0.0), (), mv)
        tok = {}

        def load_blocks(queue, name, which, c):
            p_, c_ = c * PAIRS_PER_CHUNK // MAPC, c * PAIRS_PER_CHUNK % MAPC

            def build(e):
                if name not in regs:
                    regs[name] = [e.alloc_register(f"{name}{i}") for i in range(PAIRS_PER_CHUNK)]
                return e.load(regs[name], bmap[p_:p_ + 1, which, c_:c_ + PAIRS_PER_CHUNK])
            queue.put(build)

        def gather(p):
            r = p % RING
            for j in range(PAIR):
                t = p * PAIR + j
                tok["gather", p] = PO.put(lambda e, t=t, j=j: e.indirect_dma_start(
                    slot[:, r, j, 0:ROW], None, table, bass.IndirectOffsetOnAxis(ap=gidx[:, t:t + 1].bitcast(u32), axis=0)),
                    some(tok.get(("sum", p - RING))), mg[r], 16)

        def onehots(c):
            k = c % 2
            tok["oh", c] = VE.put(lambda e: e.tensor_tensor(oh[:, k, :, :], spread(lo[:, c * CHUNK:(c + 1) * CHUNK], PARTS, CHUNK),
                                                            row1c[:, :, :], ALU.is_equal),
                                  some(tok.get(("turn", (c - 1) * PAIRS_PER_CHUNK - 1))), mv)

        def turn(p):
            c, k = p // PAIRS_PER_CHUNK, p // PAIRS_PER_CHUNK % 2
            O = OT[p % 2][:, 0:PARTS].bitcast(bf16)
            for j in range(PAIR):
                t = p * PAIR + j
                tok["turn", p] = PE.put(lambda e, t=t, j=j: e.transpose(O[:, j * PARTS:(j + 1) * PARTS], oh[:, k, :, t % CHUNK], identb[:, :]),
                                        some(tok["oh", c], tok.get(("ohT", p - 2))), mp)
            tok["ohT", p] = AC.put(lambda e: e.activation(ohT[:, p % 3, :], O, ACT.Copy), some(tok["turn", p], tok.get(("qk", p - 3))), ma)

        def qk(p):
            if p % PAIRS_PER_CHUNK == 0:
                load_blocks(PE, "pe_block", 0, p // PAIRS_PER_CHUNK)
            K, r = QK[p % 2], p % RING
            PE.put(lambda e: e.matmul(K[:, 0:PAIR * A], identf[:, :], slot[:, r, :, 0:A], start=True, stop=False),
                   some(tok["gather", p], tok.get(("e", p - 2))), mp)
            for j in range(PAIR):
                for s_ in range(3):
                    def build(e, j=j, s_=s_):
                        b = e.snap(regs["pe_block"][p % PAIRS_PER_CHUNK], min_val=0, max_val=(NB - 1) * 3 * A)
                        return e.matmul(K[:, j * A:(j + 1) * A], ohT[:, p % 3, j * PARTS:(j + 1) * PARTS],
                                        q3[:, bass.ds(b + s_ * A, A)], start=False, stop=s_ == 2 and j == PAIR - 1)
                    tok["qk", p] = PE.put(build, (tok["ohT", p],), mp)
            tok["e", p] = AC.put(lambda e: e.activation(slot[:, r, :, ROW:ROW + A], K[:, 0:PAIR * A].rearrange("p (j f) -> p j f", f=A), ACT.Tanh),
                                 (tok["qk", p],), ma)

        def scores(p):
            r, k = p % RING, p % 2
            a = VE.put(lambda e: e.tensor_tensor(ephi[:, k], slot[:, r, :, ROW:ROW + A], spread(phi[:, :], PAIR, A), ALU.mult),
                       some(tok["e", p], tok.get(("score", p - 2))), mv)
            tok["ephi", p] = a

        def scores2(p):
            k = p % 2
            tok["score", p] = VE.put(lambda e: e.tensor_reduce(score[:, p * PAIR:(p + 1) * PAIR], ephi[:, k], AX.X, ALU.add),
                                     (tok["ephi", p],), mv)
            tok["exp", p] = AC.put(lambda e: e.activation(wexp[:, p % 4, :], score[:, p * PAIR:(p + 1) * PAIR], ACT.Exp, bias=NSHIFT),
                                   some(tok["score", p], tok.get(("ohw", p - 4))), ma)

        def weigh(p):
            for j in range(PAIR):
                t = p * PAIR + j
                tok["ohw", p] = VE.put(lambda e, t=t, j=j: e.tensor_scalar(ohw[:, p % 3, j, :], row1[:, :], lof[:, t:t + 1], wexp[:, p % 4, j:j + 1],
                                                                          ALU.is_equal, ALU.mult),
                                       some(tok["exp", p], tok.get(("sum", p - 3))), mv)

        def total(p):
            M, r = SM[p % 2], p % RING
            for j in range(PAIR):
                tok["sum", p] = PE.put(lambda e, j=j: e.matmul(M[:, 0:SUMS], ohw[:, p % 3, j, :], slot[:, r, j, A:SLOT], start=j == 0, stop=j == PAIR - 1),
                                       some(tok["ohw", p], tok.get(("acc", p - 2))), mp)

        def accumulate(p):
            if p % PAIRS_PER_CHUNK == 0:
                load_blocks(VE, "ve_block", 1, p // PAIRS_PER_CHUNK)

            def build(e):
                b = e.snap(regs["ve_block"][p % PAIRS_PER_CHUNK], min_val=0, max_val=(NB - 1) * SUMS)
                return e.tensor_tensor(sums[:, bass.ds(b, SUMS)], sums[:, bass.ds(b, SUMS)], SM[p % 2][:, 0:SUMS], ALU.add)
            tok["acc", p] = VE.put(build, some(tok["sum", p], tok.get(("acc", p - 1)), z1, z2, z3), mv)

        sure_pairs = -(-E // (PAIR * PARTS))
        NC = NP // PAIRS_PER_CHUNK
        FIRST_ASKED = min(NC, -(-sure_pairs // PAIRS_PER_CHUNK) + 1)
        parts_of_pass = {k: [] for k in Q}
        landed_at = []

        def cut():
            for k, q in Q.items():
                parts_of_pass[k].append(q.items)
                q.items = []
            landed_at.append([(c, c.value) for c in mg])

        z4 = VE.put(lambda e: e.memset(score[:, (FIRST_ASKED - 1) * CHUNK:NTS], -1e30), (), mv) if FIRST_ASKED < NC else None
        STAGES = [(gather, 0), (turn, 1), (qk, 2), (scores, 3), (total, 5), (scores2, 3), (accumulate, 6), (weigh, 4)]
        for p in range(NP + 6):
            if p == NP or p < NP and p % PAIRS_PER_CHUNK == 0 and p // PAIRS_PER_CHUNK >= FIRST_ASKED:
                cut()
            if p < NP and p % PAIRS_PER_CHUNK == 0:
                onehots(p // PAIRS_PER_CHUNK)
            for stage, lag in STAGES:
                if 0 <= p - lag < NP:
                    stage(p - lag)
        cut()
        over = {k: sem(f"steps_over_{k}") for k in Q}
        ev, ep, ea = sem("end_vector"), sem("end_pool"), sem("end_scalar")
        for k, q in Q.items():
            q.put(lambda e: e.drain(), (), over[k])
        for k, q in Q.items():
            q.put(None, [(c, 1) for j, c in over.items() if j != k])
        VE.put(lambda e: e.tensor_reduce(RMAX, score[:, :], AX.X, ALU.max), (), ev)
        m1 = PO.put(lambda e: e.partition_all_reduce(GMAX, RMAX, PARTS, bass.bass_isa.ReduceOp.max), [(ev, ev.value)], ep)
        AC.put(lambda e: e.activation(TMP, GMAX, ACT.Exp, bias=NSHIFT), (m1,), ea)
        VE.put(lambda e: e.tensor_scalar(EPS9, TMP, 1e-9, None, ALU.mult), [(ea, ea.value)], ev)
        VE.put(lambda e: e.tensor_scalar(NSHIFT, GMAX, -1.0, None, ALU.mult), [(ev, ev.value)], ev)
        for k, q in Q.items():
            parts_of_pass[k].append(q.items)
        for q in Q.values():
            q.items, q.reached = [], {}
        arrive = {k: sem(f"pass_over_{k}") for k in Q if k != "sync"}
        leave = {k: sem(f"pass_next_{k}") for k in Q if k != "sync"}
        pass_sems = [mv, mp, ma, mgp, *mg, ev, ep, ea, *over.values()]

        lists.close()
        fin = scope()
        FB = 2
        FX, FR = 4, 3
        fx = sb(fin, "x_again", [PARTS, FX, FB, D], f32)
        tT = sb(fin, "sums_T", [PARTS, 2, FB, 2, PARTS], f32)
        rden = sb(fin, "one_over_weight", [PARTS, NB], f32)
        hres = sb(fin, "residual", [PARTS, FR, FB, D], f32)
        bst = sb(fin, "bn_stats", [PARTS, FR, FB, 6], f32)
        mvar = sb(fin, "mean_var", [PARTS, FR, FB, 2], f32)
        sd = sb(fin, "deviation", [PARTS, FR, 2, FB], f32)
        fo = sb(fin, "out_rows", [PARTS, 2, FB, D], f32)
        sv = sums[:, :].rearrange("p (b s) -> p b s", s=SUMS)
        V(lambda e: e.tensor_scalar(rden[:, :], sv[:, :, SUMS - 1], EPS9, None, ALU.add))
        V(lambda e: e.reciprocal(rden[:, :], rden[:, :]))
        eps = V(lambda e: e.memset(TMP, 1e-5))
        fl = [sem(f"x_again_loaded_{i}") for i in range(FX)]
        fs = [sem(f"out_stored_{i}") for i in range(2)]
        TT, NUM = [bank[0], bank[1]], [bank[2], bank[3]]
        TE = A + 1
        f_ = {}

        def split(i):
            b0 = i * FB
            n = min(FB, NB - b0)
            return b0, n, n if b0 + n < NB or LAST == PARTS else n - 1

        def f_load(i):
            b0, n, whole = split(i)
            k = i % FX
            w_ = some(f_.get(("res", i - FX)))
            if whole < n:
                w_ = [VE.put(lambda e: e.memset(fx[:, k, whole, :], 0.0), w_, ve)]
            if whole:
                f_["x", i] = SP.put(lambda e: e.dma_start(
                    fx[:, k, 0:whole, :], x[b0 * PARTS:(b0 + whole) * PARTS, :].rearrange("(b p) d -> p b d", p=PARTS)), w_, fl[k], 16)
            if whole < n:
                f_["x", i] = SP.put(lambda e: e.dma_start(fx[0:LAST, k, whole, :], x[(NB - 1) * PARTS:N, :]), w_, fl[k], 16)

        def f_turn(i):
            b0, n, _ = split(i)
            s = i % 2
            for j in range(n):
                PE.put(lambda e, j=j: e.transpose(TT[s][:, j * 256:j * 256 + PARTS], sv[:, b0 + j, 0:D], identf[:, :]), some(f_.get(("tT", i - 2))), pe)
                t = PE.put(lambda e, j=j: e.transpose(TT[s][0:TE, j * 256 + PARTS:(j + 1) * 256], sv[:, b0 + j, D:SUMS], identf[:, :]), (), pe)
            ttv = TT[s][:, 0:n * 256].rearrange("p (j a c) -> p j a c", a=2, c=PARTS)
            AC.put(lambda e: e.activation(tT[:, s, 0:n, 0, :], ttv[:, :, 0, :], ACT.Copy), some(t, f_.get(("num", i - 2))), ac)
            f_["tT", i] = AC.put(lambda e: e.activation(tT[0:TE, s, 0:n, 1, :], ttv[0:TE, :, 1, :], ACT.Copy), (), ac)

        def f_product(i):
            b0, n, _ = split(i)
            s = i % 2
            for j in range(n):
                o = NUM[s][:, j * D:(j + 1) * D]
                PE.put(lambda e, j=j, o=o: e.matmul(o, tT[:, s, j, 0, :], wy[:, :], start=True, stop=False), some(f_["tT", i], f_.get(("res", i - 2))), pe)
                f_["num", i] = PE.put(lambda e, j=j, o=o: e.matmul(o, tT[0:TE, s, j, 1, :], web[:, :], start=False, stop=True), (), pe)

        def f_residual(i):
            b0, n, _ = split(i)
            s, r, k = i % 2, i % FR, i % FX
            for j in range(n):
                f_["res", i] = VE.put(lambda e, j=j: e.scalar_tensor_tensor(
                    hres[:, r, j, :], NUM[s][:, j * D:(j + 1) * D], rden[:, b0 + j:b0 + j + 1], fx[:, k, j, :], ALU.mult, ALU.add),
                    some(f_["num", i], f_["x", i], eps, f_.get(("out", i - FR))), ve)

        def f_stats(i):
            b0, n, _ = split(i)
            r = i % FR
            for j in range(n):
                a = VE.put(lambda e, j=j: e.bn_stats(bst[:, r, j, :], hres[:, r, j, :]), some(f_["res", i], f_.get(("sd", i - FR))), ve)
            f_["bn", i] = a

        def f_aggregate(i):
            b0, n, _ = split(i)
            r = i % FR
            for j in range(n):
                a = VE.put(lambda e, j=j: e.bn_aggr(mvar[:, r, j, :], bst[:, r, j, :]), (f_["bn", i],), ve)
            f_["sd", i] = AC.put(lambda e: e.activation(sd[:, r, 0, 0:n], mvar[:, r, 0:n, 1], ACT.Sqrt, bias=TMP), (a,), ac)

        def f_invert(i):
            b0, n, _ = split(i)
            r = i % FR
            f_["inv", i] = VE.put(lambda e: e.reciprocal(sd[:, r, 1, 0:n], sd[:, r, 0, 0:n]), (f_["sd", i],), ve)

        def f_norm(i):
            b0, n, whole = split(i)
            s, r = i % 2, i % FR
            for j in range(n):
                b_ = f_["out", i] = VE.put(lambda e, j=j: e.tensor_scalar(
                    fo[:, s, j, :], hres[:, r, j, :], mvar[:, r, j, 0:1], sd[:, r, 1, j:j + 1],
                    ALU.subtract, ALU.mult), some(f_["inv", i], f_.get(("stored", i - 2))), ve)
            if whole:
                f_["stored", i] = SP.put(lambda e: e.dma_start(
                    out[b0 * PARTS:(b0 + whole) * PARTS, :].rearrange("(b p) d -> p b d", p=PARTS), fo[:, s, 0:whole, :]), (b_,), fs[s], 16)
            if whole < n:
                f_["stored", i] = SP.put(lambda e: e.dma_start(out[(NB - 1) * PARTS:N, :], fo[0:LAST, s, whole, :]), (b_,), fs[s], 16)

        NF = -(-NB // FB)
        F_STAGES = [(f_load, 0), (f_turn, 2), (f_product, 3), (f_invert, 5), (f_stats, 4), (f_residual, 3), (f_norm, 5), (f_aggregate, 4)]
        for i in range(NF + 5):
            for stage, lag in F_STAGES:
                if 0 <= i - lag < NF:
                    stage(i - lag)
        SP.put(None, [(c, c.value) for c in fs])
        after_pass = {k: q.items for k, q in Q.items()}

        def play(name, engine):
            q = Queue()
            q.items = before_pass[name]
            q.run(engine)
            reg = engine.alloc_register(f"passes_{name}")
            engine.reg_load(reg, passes[0:1, 0:1])
            used_reg = engine.alloc_register(f"pairs_used_{name}")
            engine.reg_load(used_reg, used[0:1, 0:1])
            pairs_used = engine.snap(used_reg, min_val=0, max_val=NP)
            with engine.Fori(0, engine.snap(reg, min_val=1, max_val=2)):
                first, *asked, flush, end = parts_of_pass[name]

                def run(items):
                    q.items = items
                    q.run(engine)

                def landed(at):
                    if name == "gpsimd":
                        for c, value in landed_at[at]:
                            if value:
                                engine.wait_ge(c.sem, value)

                def steps(i):
                    if i == len(asked):
                        run(flush)
                        landed(i + 1)
                        return
                    with engine.If(pairs_used > (FIRST_ASKED + i - 1) * PAIRS_PER_CHUNK):
                        run(asked[i])
                        steps(i + 1)
                    if name == "gpsimd":
                        with engine.Else():
                            landed(i)

                run(first)
                steps(0)
                run(end)
                if name == "sync":
                    for c in arrive.values():
                        engine.wait_ge(c.sem, 1)
                    for c in (*arrive.values(), *pass_sems):
                        engine.sem_clear(c.sem)
                    for c in leave.values():
                        engine.sem_inc(c.sem, 1)
                else:
                    if name == "gpsimd":
                        engine.dma_reset()
                    engine.drain().then_inc(arrive[name].sem, 1)
                    engine.wait_ge(leave[name].sem, 1)
                    engine.sem_inc(leave[name].sem, -1)
            q.items = after_pass[name]
            q.run(engine)

        block = ctx.enter_context(nc.Block())

        @block.sync
        def _(e):
            play("sync", e)

        @block.gpsimd
        def _(e):
            play("gpsimd", e)

        @block.vector
        def _(e):
            play("vector", e)

        @block.scalar
        def _(e):
            play("scalar", e)

        @block.tensor
        def _(e):
            play("tensor", e)
        fin.close()
        main.close()


_INS = ["x", "src", "dst", "L0_gnn_Wq", "L0_gnn_Wk", "L0_gnn_Wphi", "L0_gnn_Wy_w", "L0_gnn_Wy_b", "L0_gnn_We"]


def kernel(**inputs):
    import numpy as np
    import concourse.bacc as bacc
    from concourse.bass_utils import run_bass_kernel_spmd

    nc = bacc.Bacc("TRN2", target_bir_lowering=False, num_devices=1)
    arrays, args = {}, []
    for name in _INS:
        a = np.ascontiguousarray(inputs[name])
        arrays[f"in_{name}"] = a
        args.append(nc.dram_tensor(f"in_{name}", a.shape, mybir.dt.from_np(a.dtype), kind="ExternalInput").ap())
    shape = arrays["in_x"].shape
    args.append(nc.dram_tensor("out", shape, mybir.dt.float32, kind="ExternalOutput").ap())
    gnn_program(nc, *args)
    r = run_bass_kernel_spmd(nc, [arrays], core_ids=[0])
    return r.results[0]["out"]
```

```python
import concourse.bass as bass
from concourse import mybir
from contextlib import ExitStack

PARTS = 128
COLS = 64
UNIT = 4
PAIR = 2
UNITS_PER_PAIR = PAIR * PARTS // UNIT
UNITS_PER_ROW = COLS // UNIT
UNITS_PER_TILE = PARTS // UNIT
CHUNK = 16
PAIRS_PER_CHUNK = CHUNK // PAIR
LOOSE_BOUND = 30.0
FAR = 65536.0
SKIP = float(1 << 21)


class Counter:

    def __init__(self, sem):
        self.sem, self.value = sem, 0

    def add(self, by):
        self.value += by
        return (self, self.value)


class Queue:

    def __init__(self):
        self.items, self.reached = [], {}

    def put(self, build, waits=(), done=None, by=1):
        need = []
        for counter, value in waits:
            if self.reached.get(counter, 0) < value:
                self.reached[counter] = value
                need.append((counter.sem, value))
        self.items.append((need, build, done.sem if done else None, by))
        return done.add(by) if done else None

    def run(self, engine):
        for need, build, sem, by in self.items:
            for s, value in need:
                engine.wait_ge(s, value)
            made = build(engine) if build else None
            if sem is not None:
                made.then_inc(sem, by)
        self.items = []


def gnn_program(nc, x, src, dst, Wq, Wk, Wphi, Wy_w, Wy_b, We, out):
    f32, i32, u32 = mybir.dt.float32, mybir.dt.int32, mybir.dt.uint32
    bf16, f16 = mybir.dt.bfloat16, mybir.dt.float16
    ALU, ACT, AX = mybir.AluOpType, mybir.ActivationFunctionType, mybir.AxisListType

    N, D = x.shape
    E = src.shape[0]
    A = Wq.shape[1]
    NB = -(-N // PARTS)
    LAST = N - (NB - 1) * PARTS
    NT = -(-E // PARTS)
    EW = E // PARTS
    EREST = E - EW * PARTS
    ROW = A + D
    SUMS = D + A + 1
    SLOT = ROW + A + 1

    TPG = min(NT, PARTS * COLS // PARTS, (PARTS * COLS - NB * (UNIT - 1)) // PARTS)
    NG = -(-NT // TPG)
    g_tiles = [min(TPG, NT - g * TPG) for g in range(NG)]
    max_units = (E + NG * NB * (UNIT - 1)) // UNIT
    max_pairs = (max_units + NB * (UNITS_PER_PAIR - 1)) // UNITS_PER_PAIR
    NP = -(-max_pairs // PAIRS_PER_CHUNK) * PAIRS_PER_CHUNK
    NTS = NP * PAIR
    LU = NTS * UNITS_PER_TILE
    MAPC = 16
    assert NP <= PARTS * MAPC and N + 1 < 1 << 14 and NB * (UNIT - 1) < PARTS * COLS // 2
    NBL = 8
    NBH = -(-NB // NBL)
    assert TPG * NBL <= 512
    PB = 512 // NB
    GB = 4

    table = nc.dram_tensor("table", (N + 1, ROW), f32).ap()
    slist = nc.dram_tensor("sorted_list", (LU, UNIT), i32).ap()

    ctx = ExitStack()
    with ctx:
        def scope():
            return ExitStack()

        def sb(where, name, shape, dt):
            return where.enter_context(nc.sbuf_tensor(name, shape, dt))

        def sem(name):
            return Counter(ctx.enter_context(nc.semaphore(name)))

        bank = [ctx.enter_context(nc.psum_tensor(f"bank{i}", [PARTS, 512], f32)) for i in range(8)]

        row1 = sb(ctx, "row_1_to_128", [PARTS, PARTS], f32)
        part = sb(ctx, "partition_number", [PARTS, 1], f32)
        row1c = sb(ctx, "row_1_to_128_chunk", [PARTS, PARTS, CHUNK], bf16)
        identf = sb(ctx, "identity_f32", [PARTS, PARTS], f32)
        identb = sb(ctx, "identity_bf16", [PARTS, PARTS], bf16)
        before = sb(ctx, "before", [PARTS, PARTS], bf16)
        before_far = sb(ctx, "before_far", [PARTS, PARTS], bf16)
        ones = sb(ctx, "ones", [PARTS, PARTS], bf16)
        onesf = sb(ctx, "ones_f32", [1, PARTS], f32)
        wkq = sb(ctx, "wk_wq", [D, 2 * A], f32)
        wy = sb(ctx, "wy", [D, D], f32)
        web = sb(ctx, "we_bias", [A + 1, D], f32)
        phi = sb(ctx, "phi", [PARTS, A], f32)
        row0 = sb(ctx, "table_row_0", [1, ROW], f32)
        stat = sb(ctx, "stat", [PARTS, 8], f32)
        BOUND, NSHIFT, RMAX, GMAX, EPS9, TMP = (stat[:, i:i + 1] for i in range(6))
        passes = sb(ctx, "passes", [1, 1], i32)
        used = sb(ctx, "pairs_used", [1, 1], i32)
        q3 = sb(ctx, "q_parts", [PARTS, NB * 3 * A], bf16)
        bmap = sb(ctx, "pair_blocks", [PARTS, 2, MAPC], i32)

        Q = {k: Queue() for k in ("sync", "gpsimd", "vector", "scalar", "tensor")}
        SP, PO, VE, AC, PE = (Q[k] for k in ("sync", "gpsimd", "vector", "scalar", "tensor"))
        po, ve, ac, pe = sem("pool_done"), sem("vector_done"), sem("scalar_done"), sem("tensor_done")
        fence_sems = {k: sem(f"fence_{k}") for k in Q}

        def V(build, *waits):
            return VE.put(build, [(ve, ve.value), *waits] if ve.value else waits, ve)

        def fence():
            for k, q in Q.items():
                q.put(lambda e: e.drain(), (), fence_sems[k])
            for k, q in Q.items():
                q.put(None, [(c, c.value) for j, c in fence_sems.items() if j != k])

        sort, early = scope(), scope()
        blk = sb(sort, "edge_block", [PARTS, NT], bf16)
        rec_hi = sb(sort, "record_high", [PARTS, NT], f16)
        rec_lo = sb(sort, "record_low", [PARTS, NT], f32)
        rowbc = sb(sort, "row_0_to_nb_chunk", [PARTS, NB, CHUNK], bf16)
        sortd = sb(sort, "sorted_groups", [PARTS, NG, COLS], i32)
        counts = sb(sort, "tile_block_counts", [PARTS, NG, NBH * NBL], bf16)

        srcs = sb(early, "src_edges", [PARTS, NT], i32)
        dsts = sb(early, "dst_edges", [PARTS, NT], i32)
        blk_hi = sb(early, "edge_block_high", [PARTS, NT], bf16)
        blk_lo = sb(early, "edge_block_low", [PARTS, NT], bf16)
        hoth = sb(early, "block_high_onehots", [PARTS, 3, NBH, TPG], bf16)
        hotl = sb(early, "block_low_onehots", [PARTS, 3, NBL, TPG], bf16)
        rowt = sb(early, "row_0_to_nbh_tiles", [PARTS, max(NBH, NBL), TPG], bf16)
        tiles_of = sb(early, "tile_counts", [NBH, 2, TPG * NBL], bf16)
        XR = 4
        xin = sb(early, "x_in", [PARTS, XR, GB, D], f32)
        xT = sb(early, "xT", [PARTS, 2, GB * PARTS], f32)
        kst = sb(early, "k_and_q", [PARTS, XR, GB, 2 * A], f32)
        rest = sb(early, "q_rest", [PARTS, 2, GB, A], f32)
        ZU = max(z for z in range(1, 65) if LU // PARTS % z == 0)
        zeros = sb(early, "zero_units", [PARTS, ZU * UNIT], i32)
        some = lambda *w: [z for z in w if z is not None]
        el = sem("edges_loaded")
        MANY = 1 << 20
        pads = None
        if EREST:
            VE.put(lambda e: e.memset(srcs[:, EW:NT], MANY), (), ve)
            pads = VE.put(lambda e: e.memset(dsts[:, EW:NT], 0), (), ve)
        for t_, a_ in ((srcs, src), (dsts, dst)):
            SP.put(lambda e, t_=t_, a_=a_: e.dma_start(t_[:, 0:EW], a_[0:EW * PARTS].rearrange("(p c) -> p c", p=PARTS)), (), el, 16)
            if EREST:
                SP.put(lambda e, t_=t_, a_=a_: e.dma_start(t_[0:EREST, EW:NT], a_[EW * PARTS:E].rearrange("(p c) -> p c", c=1)), (pads,), el, 16)

        ld = sem("weights_loaded")
        for dst_ap, src_ap in ((wkq[:, 0:A], Wk), (wkq[:, A:2 * A], Wq), (wy[:, :], Wy_w),
                               (web[0:A, :], We), (web[A:A + 1, :], Wy_b.rearrange("(a n) -> a n", a=1)),
                               (phi[:, :], Wphi.rearrange("(a n) -> a n", a=1).to_broadcast([PARTS, A]))):
            loaded = SP.put(lambda e, d=dst_ap, s=src_ap: e.dma_start(d, s), (), ld, 16)
        tabx = sem("table_x_written")

        PO.put(lambda e: e.iota(row1[:, :], [[1, PARTS]], base=1, channel_multiplier=0,
                                allow_small_or_imprecise_dtypes=True), (), po)
        PO.put(lambda e: e.iota(part[:, :], [[0, 1]], base=1, channel_multiplier=1,
                                allow_small_or_imprecise_dtypes=True), (), po)
        iotas = PO.put(lambda e: e.iota(row1c[:, :, :], [[1, PARTS], [0, CHUNK]], base=1, channel_multiplier=0,
                                        allow_small_or_imprecise_dtypes=True), (), po)
        V(lambda e: e.tensor_scalar(identf[:, :], row1[:, :], part[:, :], None, ALU.is_equal), iotas)
        V(lambda e: e.tensor_scalar(identb[:, :], row1[:, :], part[:, :], None, ALU.is_equal))
        V(lambda e: e.tensor_scalar(before[:, :], row1[:, :], part[:, :], None, ALU.is_gt))
        V(lambda e: e.scalar_tensor_tensor(before_far[:, :], identf[:, :], FAR, before[:, :], ALU.mult, ALU.add))
        V(lambda e: e.memset(ones[:, :], 1.0))
        V(lambda e: e.memset(onesf[:, :], 1.0))
        V(lambda e: e.tensor_reduce(BOUND, phi[:, :], AX.X, ALU.add, apply_absolute_value=True), loaded)
        V(lambda e: e.tensor_scalar(NSHIFT, BOUND, -1.0, None, ALU.mult))
        V(lambda e: e.tensor_scalar(passes[:, :], BOUND[0:1, :], LOOSE_BOUND, 1.0, ALU.is_ge, ALU.add))
        consts = (ve, ve.value)
        V(lambda e: e.memset(row0[:, :], 0.0))
        V(lambda e: e.tensor_scalar(row0[:, 0:A], phi[0:1, :], 0.0, 60.0, ALU.is_lt, ALU.mult))
        row0_made = V(lambda e: e.tensor_scalar(row0[:, 0:A], row0[:, 0:A], -30.0, None, ALU.add))
        tab0 = sem("table_row_0_written")
        SP.put(lambda e: e.dma_start(table[0:1, :], row0[:, :]), (row0_made,), tab0, 16)


        def spread(col, n, m):
            return col.rearrange("p (a m) -> p a m", a=1).to_broadcast([PARTS, n, m])

        zeroed = PO.put(lambda e: e.memset(zeros[:, :], 0), (), po)
        lz = sem("list_zeroed")

        def zero_list():
            AC.put(lambda e: e.dma_start(slist.rearrange("(p r a) u -> p r (a u)", p=PARTS, a=ZU), spread(zeros[:, :], LU // PARTS // ZU, ZU * UNIT)),
                   (zeroed,), lz, 16)

        TX = 4

        def table_x(i):
            r0, r1 = N * i // TX, N * (i + 1) // TX
            if r1 > r0:
                AC.put(lambda e: e.dma_start(table[1 + r0:1 + r1, A:ROW], x[r0:r1, :]), (), tabx, 16)

        PO.put(lambda e: e.iota(rowt[:, :, :], [[1, max(NBH, NBL)], [0, TPG]], base=0, channel_multiplier=0,
                                allow_small_or_imprecise_dtypes=True), (), po)
        rows = PO.put(lambda e: e.iota(rowbc[:, :, :], [[1, NB], [0, CHUNK]], base=0, channel_multiplier=0,
                                       allow_small_or_imprecise_dtypes=True), (), po)
        S_ = srcs[:, :]
        D_ = dsts[:, :]
        tmp = sortd[:, :, :].rearrange("p g e -> p (g e)")[:, 0:NT]
        a = V(lambda e: e.tensor_scalar(tmp, S_, 7, None, ALU.logical_shift_right), (el, el.value))
        blk_made = AC.put(lambda e: e.activation(blk[:, :], tmp, ACT.Copy), (a,), ac)
        high = rec_lo[:, :].bitcast(i32)
        a = VE.put(lambda e: e.tensor_scalar(high, tmp, NBL.bit_length() - 1, None, ALU.logical_shift_right), (a,), ve)
        hi_made = AC.put(lambda e: e.activation(blk_hi[:, :], high, ACT.Copy), (a,), ac)
        V(lambda e: e.tensor_scalar(tmp, tmp, NBL - 1, None, ALU.bitwise_and), blk_made)
        lo_made = V(lambda e: e.tensor_copy(blk_lo[:, :], tmp))
        parts_made = (hi_made, lo_made)
        V(lambda e: e.tensor_scalar(S_, S_, PARTS - 1, None, ALU.bitwise_and))
        a = AC.put(lambda e: e.activation(D_, D_, ACT.Copy, scale=256.0, bias=257.0), some((el, el.value), pads), ac)
        V(lambda e: e.tensor_tensor(D_, D_, S_, ALU.add), a)
        a = V(lambda e: e.tensor_scalar(tmp, D_, 11, None, ALU.logical_shift_right))
        AC.put(lambda e: e.activation(rec_hi[:, :], tmp, ACT.Copy), (a,), ac)
        a = V(lambda e: e.tensor_scalar(D_, D_, 2047, None, ALU.bitwise_and))
        AC.put(lambda e: e.activation(rec_lo[:, :], D_, ACT.Copy), (a, hi_made), ac)

        COUNT, TURNED = [bank[4], bank[5]], [bank[6], bank[7]]
        c_ = {}
        short = V(lambda e: e.memset(counts[:, NG - 1, :], 0.0)) if g_tiles[-1] < TPG else None

        def count_onehots(g):
            k, T, a = g % 3, g_tiles[g], g * TPG
            for hot_, number, n in ((hoth, blk_hi, NBH), (hotl, blk_lo, NBL)):
                c_["hot", g] = VE.put(lambda e, h=hot_, b=number, n=n: e.tensor_tensor(
                    h[:, k, :, 0:T], spread(b[:, a:a + T], n, T), rowt[:, 0:n, 0:T], ALU.is_equal),
                    some(c_.get(("count", g - 3)), rows, *parts_made), ve)

        def count_tiles(g):
            k, T, C = g % 3, g_tiles[g], COUNT[g % 2]
            for t in range(T):
                c_["count", g] = PE.put(lambda e, t=t: e.matmul(C[0:NBH, t * NBL:(t + 1) * NBL], hoth[:, k, :, t], hotl[:, k, :, t], start=True, stop=True),
                                        some(c_["hot", g], c_.get(("tiles", g - 2))), pe)
            c_["tiles", g] = AC.put(lambda e: e.activation(tiles_of[:, g % 2, 0:T * NBL], C[0:NBH, 0:T * NBL], ACT.Copy),
                                    some(c_["count", g], c_.get(("turned", g - 2))), ac)

        def count_turn(g):
            T, C = g_tiles[g], TURNED[g % 2]
            tv = tiles_of[:, g % 2, 0:T * NBL].rearrange("h (t l) -> h l t", l=NBL)
            for l in range(NBL):
                c_["turned", g] = PE.put(lambda e, l=l: e.matmul(C[0:T, l * NBH:(l + 1) * NBH], tv[:, l, :], identb[0:NBH, 0:NBH], start=True, stop=True),
                                         some(c_["tiles", g], c_.get(("counts", g - 2)), consts), pe)
            c_["counts", g] = AC.put(lambda e: e.activation(counts[0:T, g, :].rearrange("t (h l) -> t h l", l=NBL),
                                                            C[0:T, 0:NBL * NBH].rearrange("t (l h) -> t h l", h=NBH), ACT.Copy),
                                     some(c_["turned", g], short), ac)

        xl = [sem(f"x_loaded_{i}") for i in range(XR)]
        ks = [sem(f"k_stored_{i}") for i in range(XR)]
        q3v = q3[:, :].rearrange("p (b s f) -> p b s f", s=3, f=A)
        NQ = -(-NB // GB)
        n_ = {}

        def q_split(i):
            b0 = i * GB
            n = min(GB, NB - b0)
            return i % 2, b0, n, n if b0 + n < NB or LAST == PARTS else n - 1

        def node_load(i):
            s, b0, n, whole = q_split(i)
            waits = some(n_.get(("turn", i - XR)))
            if whole < n:
                waits = [VE.put(lambda e: e.memset(xin[:, i % XR, whole, :], 0.0), waits, ve)]
            if whole:
                n_["load", i] = SP.put(lambda e: e.dma_start(
                    xin[:, i % XR, 0:whole, :], x[b0 * PARTS:(b0 + whole) * PARTS, :].rearrange("(b p) d -> p b d", p=PARTS)),
                    waits, xl[i % XR], 16)
            if whole < n:
                n_["load", i] = SP.put(lambda e: e.dma_start(xin[0:LAST, i % XR, whole, :], x[(NB - 1) * PARTS:N, :]), waits, xl[i % XR], 16)

        def node_turn(i):
            s, b0, n, whole = q_split(i)
            X = bank[s]
            for j in range(n):
                n_["turn", i] = PE.put(lambda e, j=j: e.transpose(X[:, j * PARTS:(j + 1) * PARTS], xin[:, i % XR, j, :], identf[:, :]),
                                       some(n_["load", i], n_.get(("xT", i - 2)), consts), pe)
            n_["xT", i] = AC.put(lambda e: e.activation(xT[:, s, 0:n * PARTS], X[:, 0:n * PARTS], ACT.Copy),
                                 some(n_["turn", i], n_.get(("kq", i - 2))), ac)

        def node_product(i):
            s, b0, n, whole = q_split(i)
            B_ = bank[2 + s]
            for j in range(n):
                n_["kq", i] = PE.put(lambda e, j=j: e.matmul(B_[:, j * 2 * A:(j + 1) * 2 * A], xT[:, s, j * PARTS:(j + 1) * PARTS],
                                                             wkq[:, :], start=True, stop=True),
                                     some(n_["xT", i], n_.get(("kq_out", i - 2)), loaded), pe)
            kq = B_[:, 0:n * 2 * A].rearrange("p (b c) -> p b c", c=2 * A)
            n_["kq_out", i] = AC.put(lambda e: e.activation(kst[:, i % XR, 0:n, :], kq, ACT.Copy),
                                     some(n_["kq", i], n_.get(("k_stored", i - XR)), n_.get(("q", i - XR))), ac)
            for w0, w, r in [(0, whole, PARTS)] * (whole > 0) + [(whole, 1, LAST)] * (whole < n):
                r0 = 1 + (b0 + w0) * PARTS
                n_["k_stored", i] = AC.put(lambda e, w0=w0, w=w, r=r, r0=r0: e.dma_start(
                    table[r0:r0 + (w - 1) * PARTS + r, 0:A].rearrange("(b p) f -> p b f", p=r),
                    kst[0:r, i % XR, w0:w0 + w, 0:A]), (n_["kq_out", i],), ks[i % XR], 16)

        def node_q0(i):
            s, b0, n, whole = q_split(i)
            n_["q0", i] = AC.put(lambda e: e.activation(q3v[:, b0:b0 + n, 0, :], kst[:, i % XR, 0:n, A:2 * A], ACT.Copy), (n_["kq_out", i],), ac)

        def node_q1(i):
            s, b0, n, whole = q_split(i)
            n_["q", i] = VE.put(lambda e: e.tensor_tensor(rest[:, s, 0:n, :], kst[:, i % XR, 0:n, A:2 * A], q3v[:, b0:b0 + n, 0, :], ALU.subtract),
                                some(n_["q0", i], n_.get(("q2", i - 2))), ve)
            n_["q1", i] = AC.put(lambda e: e.activation(q3v[:, b0:b0 + n, 1, :], rest[:, s, 0:n, :], ACT.Copy), (n_["q", i],), ac)

        def node_q2(i):
            s, b0, n, whole = q_split(i)
            n_["q2", i] = VE.put(lambda e: e.tensor_tensor(q3v[:, b0:b0 + n, 2, :], rest[:, s, 0:n, :], q3v[:, b0:b0 + n, 1, :], ALU.subtract),
                                 (n_["q1", i],), ve)

        N_STAGES = [(node_load, 0), (node_turn, XR - 1), (node_product, XR), (node_q0, XR), (node_q1, XR + 1), (node_q2, XR + 2)]
        GPS = -(-NG // (NQ + XR + 2))
        C_STAGES = [(count_onehots, 0), (count_turn, 3), (count_tiles, 1)]
        STEPS = max(-(-(NG + 3) // GPS), NQ + XR + 2)
        for i in range(STEPS):
            for stage, lag in N_STAGES:
                if 0 <= i - lag < NQ:
                    stage(i - lag)
            for g in range(i * GPS, (i + 1) * GPS):
                for stage, lag in C_STAGES:
                    if 0 <= g - lag < NG:
                        stage(g - lag)
            if 1 <= i <= TX:
                table_x(i - 1)
            if i == 0:
                zero_list()
        for i in range(STEPS, TX + 1):
            table_x(i - 1)

        SP.put(None, [(c, c.value) for c in (*xl, *ks)])
        AC.put(None, [(lz, 16)])
        fence()
        early.close()

        NE = NB + 1
        UPG = PARTS * UNITS_PER_ROW
        dest = sb(sort, "unit_destinations", [PARTS, NG * UNITS_PER_ROW], i32)
        base = sb(sort, "base_parts", [PARTS, 2, NG, NB], bf16)
        units = sb(sort, "run_units", [PARTS, NG, NB], f16)
        starts = sb(sort, "run_starts", [PARTS, NG, NB + 1], f16)
        V(lambda e: e.memset(starts[:, :, 0:1], 0.0))
        plan = scope()
        basei = sb(plan, "base_int", [PARTS, 2, 3, PB, NB], i32)
        toti = sb(plan, "run_totals", [PARTS, 2, PB, NB], i32)
        unit_row = sb(plan, "unit_number_row", [PARTS, UPG], f16)
        unit_no = sb(plan, "unit_number", [PARTS, UNITS_PER_ROW], f32)
        ge = sb(plan, "unit_at_or_past_start", [PARTS, 2, UPG], f16)
        map_ge = sb(plan, "pair_past_block", [PARTS, MAPC, NB], bf16)
        stepi = sb(plan, "steps_int", [PARTS, 3, NG], i32)
        steph = sb(plan, "step_parts", [PARTS, NG, 2], f16)
        destf = sb(plan, "unit_destinations_f32", [PARTS, NG * UNITS_PER_ROW], f32)
        pair_no = sb(plan, "pair_number", [PARTS, MAPC], f32)
        bmf = sb(plan, "pair_block", [PARTS, MAPC], f32)
        minus = sb(plan, "minus_the_one_before", [PARTS, PARTS], f32)
        rowp = sb(plan, "row_block_pairs", [PARTS, 3, NB], f32)
        colf = sb(plan, "col_starts_units", [PARTS, 6, NG], f32)
        colp = sb(plan, "col_block_pairs", [PARTS, 4], f32)
        colpi = sb(plan, "col_block_pairs_int", [PARTS, 1], i32)
        colph = sb(plan, "col_block_pairs_f16", [PARTS, 1], f16)
        PO.put(lambda e: e.iota(unit_row[:, :], [[1, UPG]], base=0, channel_multiplier=0,
                                allow_small_or_imprecise_dtypes=True), (), po)
        PO.put(lambda e: e.iota(unit_no[:, :], [[1, UNITS_PER_ROW]], base=0, channel_multiplier=UNITS_PER_ROW,
                                allow_small_or_imprecise_dtypes=True), (), po)
        UNIT_BITS, UPP_BITS = UNIT.bit_length() - 1, UNITS_PER_PAIR.bit_length() - 1
        nos = PO.put(lambda e: e.iota(pair_no[:, :], [[1, MAPC]], base=0, channel_multiplier=MAPC,
                                      allow_small_or_imprecise_dtypes=True), (), po)
        assert UNIT == 1 << UNIT_BITS and UNITS_PER_PAIR == 1 << UPP_BITS
        TOTS, BASES = [bank[6], bank[0]], [bank[7], bank[1]]
        b_ = {}
        counted = (ac, ac.value)
        for n, g0 in enumerate(range(0, NG, PB)):
            k, m = n % 2, min(PB, NG - g0)
            flat_c = counts[0:TPG, g0:g0 + m, 0:NB]
            T_, B_ = TOTS[k], BASES[k]
            v3 = lambda ap, m=m: ap[:, 0:m * NB].rearrange("p (g b) -> p g b", b=NB)
            a = PE.put(lambda e, f=flat_c, m=m, T_=T_: e.matmul(T_[:, 0:m * NB], ones[0:TPG, :], f, start=True, stop=True), some(counted, b_.get(("tot", n - 2))), pe)
            b = PE.put(lambda e, f=flat_c, m=m, B_=B_: e.matmul(B_[0:TPG, 0:m * NB], before[0:TPG, 0:TPG], f, start=True, stop=True), some(b_.get(("base", n - 2))), pe)
            a = b_["tot", n] = AC.put(lambda e, m=m, v3=v3, k=k, T_=T_: e.activation(toti[:, k, 0:m, :], v3(T_[:, :]), ACT.Copy, bias=float(UNIT - 1)),
                                      some(a, b_.get(("starts", n - 2)), b_.get(("units", n - 2))), ac)
            a = VE.put(lambda e, m=m, k=k: e.tensor_scalar(toti[:, k, 0:m, :], toti[:, k, 0:m, :], UNIT_BITS, None, ALU.logical_shift_right), (a,), ve)
            b_["units", n] = AC.put(lambda e, m=m, g0=g0, k=k: e.activation(units[:, g0:g0 + m, :], toti[:, k, 0:m, :], ACT.Copy), (a,), ac)
            for g in range(g0, g0 + m):
                b_["starts", n] = VE.put(lambda e, g=g, g0=g0, k=k: e.tensor_tensor_scan(
                    starts[:, g, 1:NE], toti[:, k, g - g0, :], toti[:, k, g - g0, :], 0.0, ALU.add, ALU.bypass), (a,), ve)
            b_["base", n] = V(lambda e, m=m, g0=g0, v3=v3, k=k, B_=B_: e.scalar_tensor_tensor(
                basei[0:TPG, k, 0, 0:m, :], starts[0:TPG, g0:g0 + m, 0:NB], float(UNIT), v3(B_[0:TPG, :]), ALU.mult, ALU.add),
                *some(b, b_.get(("parts", n - 2))))
            a = b_["base", n]
            for part_, mask in ((1, -PARTS), (2, PARTS - 1)):
                a2 = VE.put(lambda e, m=m, k=k, part_=part_, mask=mask: e.tensor_scalar(
                    basei[0:TPG, k, part_, 0:m, :], basei[0:TPG, k, 0, 0:m, :], mask, None, ALU.bitwise_and), (a,), ve)
            b_["parts", n] = AC.put(lambda e, m=m, g0=g0, k=k: e.activation(base[0:TPG, :, g0:g0 + m, :], basei[0:TPG, k, 1:3, 0:m, :], ACT.Copy), (a2,), ac)
        TOT, BASE = bank[6], bank[7]
        tot_free = base_free = b_["parts", n]
        COLB = bank[4]
        for g in range(NG):
            PE.put(lambda e, g=g: e.matmul(COLB[0:NE, g:g + 1], starts[0:1, g, :], ones[0:1, 0:1], start=True, stop=True), [(ve, ve.value), base_free], pe)
            a = PE.put(lambda e, g=g: e.matmul(COLB[0:NB, NG + g:NG + g + 1], units[0:1, g, :], ones[0:1, 0:1], start=True, stop=True), (), pe)
        cstart, cunit, cupto, cdelta, cstep = (colf[:, i, :] for i in range(5))
        V(lambda e: e.tensor_copy(cstart[0:NE], COLB[0:NE, 0:NG]), a)
        V(lambda e: e.tensor_copy(cunit[0:NB], COLB[0:NB, NG:2 * NG]))
        V(lambda e: e.tensor_tensor_scan(cupto[0:NB], cunit[0:NB], cunit[0:NB], 0.0, ALU.add, ALU.bypass))
        V(lambda e: e.tensor_scalar(colpi[0:NB, :], cupto[0:NB, NG - 1:NG], float(UNITS_PER_PAIR - 1), None, ALU.add))
        V(lambda e: e.tensor_scalar(colpi[0:NB, :], colpi[0:NB, :], UPP_BITS, None, ALU.logical_shift_right))
        a = V(lambda e: e.tensor_copy(colph[0:NB, :], colpi[0:NB, :]))
        a = PE.put(lambda e: e.matmul(BASE[0:NB, 0:1], before[0:NB, 0:NB], colph[0:NB, :], start=True, stop=True), (a, base_free), pe)
        V(lambda e: e.tensor_scalar(colp[0:NB, 0:1], BASE[0:NB, 0:1], float(UNITS_PER_PAIR), None, ALU.mult), a)
        V(lambda e: e.tensor_tensor(cdelta[0:NB], cupto[0:NB], cunit[0:NB], ALU.subtract))
        V(lambda e: e.tensor_tensor(cdelta[0:NB], cdelta[0:NB], cstart[0:NB], ALU.subtract))
        V(lambda e: e.tensor_scalar(cdelta[0:NB], cdelta[0:NB], colp[0:NB, 0:1], None, ALU.add))
        V(lambda e: e.tensor_scalar(minus[:, :], row1[:, :], -1.0, part[:, :], ALU.add, ALU.is_equal))
        a = V(lambda e: e.tensor_tensor(minus[:, :], identf[:, :], minus[:, :], ALU.subtract))
        a = PE.put(lambda e: e.matmul(TOT[0:NE, 0:NG], minus[0:NB, 0:NE], cdelta[0:NB], start=True, stop=True), (a, tot_free), pe)
        V(lambda e: e.tensor_scalar(colp[:, 1:2], part[:, :], float(NE), SKIP, ALU.is_equal, ALU.mult))
        V(lambda e: e.tensor_scalar(cstep[0:NE], TOT[0:NE, 0:NG], colp[0:NE, 1:2], None, ALU.add), a)
        V(lambda e: e.tensor_copy(stepi[0:NE, 0, :], cstep[0:NE]))
        V(lambda e: e.tensor_scalar(stepi[0:NE, 1, :], stepi[0:NE, 0, :], 2047, None, ALU.bitwise_and))
        V(lambda e: e.tensor_scalar(stepi[0:NE, 2, :], stepi[0:NE, 0, :], 11, None, ALU.arith_shift_right))
        V(lambda e: e.tensor_copy(steph[0:NE, :, :].rearrange("p g s -> p s g"), stepi[0:NE, 1:3, :]))
        step_made = ve.value
        GH = 512 // (2 * UNITS_PER_ROW)
        DEST = bank[0:4]
        assert NG <= 4 * GH and UPG <= 2048
        ge_free = [None] * 2
        for g in range(NG):
            k = g % 2
            a = VE.put(lambda e, g=g, k=k: e.tensor_scalar(ge[0:NE, k, :], unit_row[0:NE, :], cstart[0:NE, g:g + 1], None, ALU.is_ge),
                       some(ge_free[k], nos, (ve, step_made)), ve)
            gv = ge[0:NE, k, :].rearrange("b (p j) -> b p j", j=UNITS_PER_ROW)
            for j in range(UNITS_PER_ROW):
                o = 2 * (g % GH * UNITS_PER_ROW + j)
                ge_free[k] = PE.put(lambda e, g=g, j=j, o=o, gv=gv: e.matmul(
                    DEST[g // GH][:, o:o + 2], gv[:, :, j], steph[0:NE, g, :], start=True, stop=True), (a,), pe)
        for h in range(-(-NG // GH)):
            m = min(GH, NG - h * GH)
            dv = DEST[h][:, 0:m * UNITS_PER_ROW * 2].rearrange("p (g j s) -> p g j s", g=m, s=2)
            df = destf[:, h * GH * UNITS_PER_ROW:(h * GH + m) * UNITS_PER_ROW].rearrange("p (g j) -> p g j", g=m)
            di = dest[:, h * GH * UNITS_PER_ROW:(h * GH + m) * UNITS_PER_ROW].rearrange("p (g j) -> p g j", g=m)
            V(lambda e, dv=dv, df=df, m=m: e.scalar_tensor_tensor(df, dv[:, :, :, 1], 2048.0, spread(unit_no[:, :], m, UNITS_PER_ROW), ALU.mult, ALU.add),
              *some(*ge_free))
            V(lambda e, dv=dv, df=df, di=di: e.tensor_tensor(di, df, dv[:, :, :, 0], ALU.add))
        tot, pairs, pend = (rowp[:, i, :] for i in range(3))
        toti2 = toti[:, 0, 0, :]
        V(lambda e: e.tensor_reduce(tot, units[:, :, :].rearrange("p g b -> p b g"), AX.X, ALU.add))
        V(lambda e: e.tensor_scalar(toti2, tot, float(UNITS_PER_PAIR - 1), None, ALU.add))
        V(lambda e: e.tensor_scalar(toti2, toti2, UPP_BITS, None, ALU.logical_shift_right))
        V(lambda e: e.tensor_copy(pairs, toti2))
        V(lambda e: e.tensor_tensor_scan(pend, pairs, pairs, 0.0, ALU.add, ALU.bypass))
        V(lambda e: e.tensor_copy(used[:, :], pend[0:1, NB - 1:NB]))
        V(lambda e: e.tensor_tensor(map_ge[:, :, :], pair_no[:, :].rearrange("p (j a) -> p j a", a=1).to_broadcast([PARTS, MAPC, NB]),
                                    spread(pend, MAPC, NB), ALU.is_ge), nos)
        V(lambda e: e.tensor_reduce(bmf[:, :], map_ge[:, :, :], AX.X, ALU.add))
        V(lambda e: e.tensor_scalar(bmf[:, :], bmf[:, :], float(NB - 1), None, ALU.min))
        V(lambda e: e.tensor_scalar(bmap[:, 0, :], bmf[:, :], float(3 * A), None, ALU.mult))
        V(lambda e: e.tensor_scalar(bmap[:, 1, :], bmf[:, :], float(SUMS), None, ALU.mult))
        fence()
        plan.close()

        late = scope()
        NHC = -(-TPG // CHUNK)
        hot = sb(late, "block_onehots", [PARTS, 2, NHC, NB, CHUNK], bf16)
        hotr = sb(late, "row_onehots", [PARTS, 2, PARTS, CHUNK], bf16)
        hotc = sb(late, "col_onehots", [PARTS, 2, COLS, CHUNK], bf16)
        recc = sb(late, "col_records", [PARTS, 2, 2, COLS, CHUNK], f16)
        pos = sb(late, "places", [PARTS, 2, TPG], f32)
        posi = sb(late, "places_int", [PARTS, TPG], i32)
        prc = sb(late, "place_row_col_int", [PARTS, 2, TPG], i32)
        prow = sb(late, "place_row", [PARTS, 2, TPG], bf16)
        pcol = sb(late, "place_col", [PARTS, 2, TPG], bf16)
        shi = sb(late, "record_high_out", [PARTS, COLS], f32)
        relu = sb(late, "relu_out", [PARTS, 4, NB], bf16)
        near = sb(late, "one_minus_far", [PARTS, 1], f32)
        bias_of = sb(late, "place_bias", [PARTS, TPG], f32)

        def scalar_has(g, c, t0):
            return t0 == c * CHUNK and c < NHC - 1

        V(lambda e: e.memset(bias_of[:, :], -FAR))
        for c in range(NHC - 1):
            V(lambda e, t0=c * CHUNK: e.memset(bias_of[:, t0:t0 + min(PB, CHUNK)], -1.0))
        near_made = V(lambda e: e.memset(near[:, :], 1.0 - FAR))
        relu_n, relu_done, summed = [0], [None] * 4, {}
        hot_made, hot_free = {}, {}

        def make_hot(g, c):
            m = min(CHUNK, g_tiles[g] - c * CHUNK)
            a = g * TPG + c * CHUNK
            hot_made[g, c] = VE.put(lambda e: e.tensor_tensor(
                hot[:, g % 2, c, :, 0:m], spread(blk[:, a:a + m], NB, m), rowbc[:, :, 0:m], ALU.is_equal),
                some(hot_free.get((g - 2, c))), ve)

        PL = {VE: [bank[0], bank[1], bank[2], bank[7]], AC: [bank[3], bank[4]]}
        pl_free = {VE: [None] * 4, AC: [None] * 2}
        pl_n = {VE: 0, AC: 0}
        split_done, prow_free = {}, {}

        def place(g, c):
            T = min(g_tiles[g], (c + 1) * CHUNK)
            for t0 in range(c * CHUNK, T, PB):
                m = min(PB, T - t0)
                E_ = AC if scalar_has(g, c, t0) else VE
                k = pl_n[E_] % len(PL[E_])
                pl_n[E_] += 1
                P = PL[E_][k]
                for t in range(t0, t0 + m):
                    o = P[:, (t - t0) * NB:(t - t0 + 1) * NB]
                    sel = identb[0:TPG, t:t + 1].to_broadcast([TPG, PARTS])
                    PE.put(lambda e, o=o, sel=sel: e.matmul(o, sel, base[0:TPG, 0, g, :], start=True, stop=False),
                           some(pl_free[E_][k]), pe)
                    PE.put(lambda e, o=o, sel=sel: e.matmul(o, sel, base[0:TPG, 1, g, :], start=False, stop=False), (), pe)
                    placed = PE.put(lambda e, o=o, t=t: e.matmul(o, before_far[:, :], hot[:, g % 2, c, :, t - c * CHUNK], start=False, stop=True),
                                    (hot_made[g, c],), pe)
                if E_ is AC:
                    for t in range(t0, t0 + m):
                        w = relu_n[0] % len(relu_done)
                        relu_n[0] += 1
                        pl_free[AC][k] = relu_done[w] = AC.put(lambda e, P=P, t=t, t0=t0, w=w: e.activation(
                            relu[:, w, :], P[:, (t - t0) * NB:(t - t0 + 1) * NB], ACT.Relu, bias=near[:, :], accum_out=pos[:, g % 2, t:t + 1]),
                            some(placed, split_done.get(g - 2), relu_done[w], near_made), ac)
                    summed[g] = pl_free[AC][k]
                    continue
                pl_free[VE][k] = VE.put(lambda e, P=P, t0=t0, m=m: e.tensor_reduce(
                    pos[:, g % 2, t0:t0 + m], P[:, 0:m * NB].rearrange("p (t b) -> p t b", b=NB), AX.X, ALU.max),
                    some(placed, split_done.get(g - 2)), ve)
            hot_free[g, c] = placed

        def split_places(g):
            T = g_tiles[g]
            V(lambda e: e.tensor_tensor(posi[:, 0:T], pos[:, g % 2, 0:T], bias_of[:, 0:T], ALU.add), *some(summed.get(g)))
            V(lambda e: e.tensor_scalar(prc[:, 0, 0:T], posi[:, 0:T], COLS.bit_length() - 1, None, ALU.arith_shift_right))
            V(lambda e: e.tensor_scalar(prc[:, 1, 0:T], posi[:, 0:T], COLS - 1, None, ALU.bitwise_and))
            V(lambda e: e.tensor_scalar(prow[:, g % 2, 0:T], prc[:, 0, 0:T], 1.0, None, ALU.add))
            split_done[g] = V(lambda e: e.tensor_scalar(pcol[:, g % 2, 0:T], prc[:, 1, 0:T], 1.0, None, ALU.add))

        OUTP = [bank[5], bank[6]]
        outp_free = [None] * 2
        n_chunk = [0]
        rec_free, rec_made, gather_hi = [None] * 2, {}, {}
        move = sem("units_moved")

        def make_records(g, c):
            m = min(CHUNK, g_tiles[g] - c * CHUNK)
            a = g * TPG + c * CHUNK
            cols = slice(c * CHUNK, c * CHUNK + m)
            k = n_chunk[0] % 2
            n_chunk[0] += 1
            b = VE.put(lambda e: e.tensor_tensor(hotc[:, k, :, 0:m], spread(pcol[:, g % 2, cols], COLS, m), row1c[:, 0:COLS, 0:m], ALU.is_equal),
                       some(rec_free[k], split_done[g]), ve)
            VE.put(lambda e: e.tensor_tensor(hotr[:, k, :, 0:m], spread(prow[:, g % 2, cols], PARTS, m), row1c[:, :, 0:m], ALU.is_equal), (), ve)
            hi = VE.put(lambda e: e.tensor_tensor(recc[:, k, 0, :, 0:m], hotc[:, k, :, 0:m], spread(rec_hi[:, a:a + m], COLS, m), ALU.mult), (b,), ve)
            for t in range(m):
                rec_made[g, c] = AC.put(lambda e, t=t: e.activation(recc[:, k, 1, :, t], hotc[:, k, :, t], ACT.Copy, scale=rec_lo[:, a + t:a + t + 1]),
                             some(b, rec_free[k]), ac)
            rec_made[g, c] = (rec_made[g, c], hi, k)

        def add_records(g, c):
            T = g_tiles[g]
            O = OUTP[g % 2]
            lo_, hi, k = rec_made[g, c]
            for t in range(min(CHUNK, T - c * CHUNK)):
                last = PE.put(lambda e, t=t: e.matmul(O[:, 0:2 * COLS], hotr[:, k, :, t], recc[:, k, :, :, t],
                                                      start=c + t == 0, stop=c * CHUNK + t == T - 1), some(hi, lo_, outp_free[g % 2]), pe)
            rec_free[k] = last
            if c == -(-T // CHUNK) - 1:
                gather_hi[g] = AC.put(lambda e: e.activation(shi[:, :], O[:, 0:COLS], ACT.Copy, scale=2048.0),
                                      some(last, outp_free[(g - 1) % 2]), ac)

        def merge_and_move(g):
            O = OUTP[g % 2]
            done = outp_free[g % 2] = VE.put(lambda e: e.tensor_tensor(sortd[:, g, :], shi[:, :], O[:, COLS:2 * COLS], ALU.add), (gather_hi[g],), ve)
            for j in range(UNITS_PER_ROW):
                o = g * UNITS_PER_ROW + j
                PO.put(lambda e, j=j, o=o: e.indirect_dma_start(
                    slist, bass.IndirectOffsetOnAxis(ap=dest[:, o:o + 1].bitcast(u32), axis=0),
                    sortd[:, g, j * UNIT:(j + 1) * UNIT], None, bounds_check=LU - 1, oob_is_err=False), (done,), move, 16)

        owed = []

        def pay():
            for g_, c_ in owed:
                add_records(g_, c_)
                if (c_ + 1) * CHUNK >= g_tiles[g_]:
                    whole_groups.append(g_)
            owed.clear()

        whole_groups = []
        for g in range(-1, NG + 1):
            for c in range(NHC):
                made = 0 <= g - 1 and c * CHUNK < g_tiles[g - 1]
                if made:
                    make_records(g - 1, c)
                if 0 <= g < NG and c * CHUNK < g_tiles[g]:
                    place(g, c)
                if g + 1 < NG and c * CHUNK < g_tiles[g + 1]:
                    make_hot(g + 1, c)
                for w in whole_groups:
                    merge_and_move(w)
                whole_groups.clear()
                if made:
                    pay()
                    owed.append((g - 1, c))
            if 0 <= g < NG:
                split_places(g)
        pay()
        merge_and_move(NG - 1)
        PO.put(None, [(move, move.value)])
        fence()
        late.close()
        sort.close()

        main = scope()
        sums = sb(main, "block_sums", [PARTS, NB * SUMS], f32)
        lists = scope()
        gidx = sb(lists, "dst_rows", [PARTS, NTS], i32)
        lo = sb(lists, "src_in_block", [PARTS, NTS], bf16)
        lof = sb(lists, "src_in_block_f32", [PARTS, NTS], f32)
        score = sb(lists, "scores", [PARTS, NTS], f32)
        RING = 6
        slot = sb(lists, "gathered", [PARTS, RING, PAIR, SLOT], f32)
        oh = sb(lists, "src_onehots", [PARTS, 2, PARTS, CHUNK], bf16)
        ohT = sb(lists, "src_onehots_T", [PARTS, 3, PAIR * PARTS], bf16)
        ohw = sb(lists, "weighted_onehots", [PARTS, 3, PAIR, PARTS], f32)
        ephi = sb(lists, "e_times_phi", [PARTS, 2, PAIR, A], f32)
        wexp = sb(lists, "edge_weight", [PARTS, 4, PAIR], f32)
        rows_sb = sums[:, 0:-(-NTS // PARTS) * PARTS]
        vi = score[:, :].bitcast(i32)
        NR = -(-NTS // PARTS)
        rw, rrest = NTS // PARTS, NTS % PARTS
        ll = sem("list_loaded")
        flat = slist.rearrange("(t a) u -> t (a u)", a=UNITS_PER_TILE)
        if rrest:
            z = VE.put(lambda e: e.memset(rows_sb[:, rw * PARTS:NR * PARTS], 0.0), (), ve)
            SP.put(lambda e: e.dma_start(rows_sb[0:rrest, rw * PARTS:NR * PARTS].bitcast(i32), flat[rw * PARTS:NTS, :]), (z,), ll, 16)
        if rw:
            SP.put(lambda e: e.dma_start(rows_sb[:, 0:rw * PARTS].rearrange("p (k e) -> p k e", e=PARTS).bitcast(i32),
                                         flat[0:rw * PARTS, :].rearrange("(k p) e -> p k e", p=PARTS)), (), ll, 16)
        half = NR // 2 * PARTS
        as_float = [V(lambda e: e.tensor_copy(rows_sb[:, half:], rows_sb[:, half:].bitcast(i32)), (ll, ll.value))]
        if half:
            as_float.append(AC.put(lambda e: e.activation(rows_sb[:, 0:half], rows_sb[:, 0:half].bitcast(i32), ACT.Copy), [(ll, ll.value)], ac))
        LB = [bank[4], bank[5], bank[6], bank[7]]
        lb_free = [None] * 4
        turned_rows = [None] * 2
        for i in range(0, NR, 4):
            k = i // 4 % 4
            n = min(4, NR - i)
            for j in range(n):
                t = PE.put(lambda e, i=i, j=j, k=k: e.transpose(LB[k][:, j * PARTS:(j + 1) * PARTS],
                           rows_sb[:, (i + j) * PARTS:(i + j + 1) * PARTS], identf[:, :]), some(lb_free[k], *as_float), pe)
            w = min(n * PARTS, NTS - i * PARTS)
            if k % 2:
                lb_free[k] = turned_rows[1] = AC.put(lambda e, i=i, k=k, w=w: e.activation(vi[:, i * PARTS:i * PARTS + w], LB[k][:, 0:w], ACT.Copy), (t,), ac)
            else:
                lb_free[k] = turned_rows[0] = VE.put(lambda e, i=i, k=k, w=w: e.tensor_copy(vi[:, i * PARTS:i * PARTS + w], LB[k][:, 0:w]), (t,), ve)
        V(lambda e: e.tensor_scalar(gidx[:, :], vi, 8, None, ALU.logical_shift_right), *some(*turned_rows))
        a = V(lambda e: e.tensor_scalar(vi, vi, 255, None, ALU.bitwise_and))
        AC.put(lambda e: e.activation(lof[:, :], vi, ACT.Copy), (a,), ac)
        V(lambda e: e.tensor_copy(lo[:, :], vi))
        V(lambda e: e.memset(slot[:, :, :, SLOT - 1:SLOT], 1.0))
        SP.put(None, [(tab0, 16)])
        AC.put(None, [(tabx, tabx.value)])
        fence()
        before_pass = {k: q.items for k, q in Q.items()}
        for q in Q.values():
            q.items, q.reached = [], {}

        mv, mp, ma, mg = sem("m_vector"), sem("m_tensor"), sem("m_scalar"), [sem(f"m_gathered_{i}") for i in range(RING)]
        mgp = sem("m_pool")
        QK, OT, SM = [bank[0], bank[1]], [bank[2], bank[3]], [bank[4], bank[5]]
        regs = {}
        H3 = NB * SUMS // 3
        z1 = VE.put(lambda e: e.memset(sums[:, 0:H3], 0.0), (), mv)
        z2 = PO.put(lambda e: e.memset(sums[:, H3:2 * H3], 0.0), (), mgp)
        z3 = VE.put(lambda e: e.memset(sums[:, 2 * H3:NB * SUMS], 0.0), (), mv)
        tok = {}

        def load_blocks(queue, name, which, c):
            p_, c_ = c * PAIRS_PER_CHUNK // MAPC, c * PAIRS_PER_CHUNK % MAPC

            def build(e):
                if name not in regs:
                    regs[name] = [e.alloc_register(f"{name}{i}") for i in range(PAIRS_PER_CHUNK)]
                return e.load(regs[name], bmap[p_:p_ + 1, which, c_:c_ + PAIRS_PER_CHUNK])
            queue.put(build)

        def gather(p):
            r = p % RING
            for j in range(PAIR):
                t = p * PAIR + j
                tok["gather", p] = PO.put(lambda e, t=t, j=j: e.indirect_dma_start(
                    slot[:, r, j, 0:ROW], None, table, bass.IndirectOffsetOnAxis(ap=gidx[:, t:t + 1].bitcast(u32), axis=0)),
                    some(tok.get(("sum", p - RING))), mg[r], 16)

        def onehots(c):
            k = c % 2
            tok["oh", c] = VE.put(lambda e: e.tensor_tensor(oh[:, k, :, :], spread(lo[:, c * CHUNK:(c + 1) * CHUNK], PARTS, CHUNK),
                                                            row1c[:, :, :], ALU.is_equal),
                                  some(tok.get(("turn", (c - 1) * PAIRS_PER_CHUNK - 1))), mv)

        def turn(p):
            c, k = p // PAIRS_PER_CHUNK, p // PAIRS_PER_CHUNK % 2
            O = OT[p % 2][:, 0:PARTS].bitcast(bf16)
            for j in range(PAIR):
                t = p * PAIR + j
                tok["turn", p] = PE.put(lambda e, t=t, j=j: e.transpose(O[:, j * PARTS:(j + 1) * PARTS], oh[:, k, :, t % CHUNK], identb[:, :]),
                                        some(tok["oh", c], tok.get(("ohT", p - 2))), mp)
            tok["ohT", p] = AC.put(lambda e: e.activation(ohT[:, p % 3, :], O, ACT.Copy), some(tok["turn", p], tok.get(("qk", p - 3))), ma)

        def qk(p):
            if p % PAIRS_PER_CHUNK == 0:
                load_blocks(PE, "pe_block", 0, p // PAIRS_PER_CHUNK)
            K, r = QK[p % 2], p % RING
            PE.put(lambda e: e.matmul(K[:, 0:PAIR * A], identf[:, :], slot[:, r, :, 0:A], start=True, stop=False),
                   some(tok["gather", p], tok.get(("e", p - 2))), mp)
            for j in range(PAIR):
                for s_ in range(3):
                    def build(e, j=j, s_=s_):
                        b = e.snap(regs["pe_block"][p % PAIRS_PER_CHUNK], min_val=0, max_val=(NB - 1) * 3 * A)
                        return e.matmul(K[:, j * A:(j + 1) * A], ohT[:, p % 3, j * PARTS:(j + 1) * PARTS],
                                        q3[:, bass.ds(b + s_ * A, A)], start=False, stop=s_ == 2 and j == PAIR - 1)
                    tok["qk", p] = PE.put(build, (tok["ohT", p],), mp)
            tok["e", p] = AC.put(lambda e: e.activation(slot[:, r, :, ROW:ROW + A], K[:, 0:PAIR * A].rearrange("p (j f) -> p j f", f=A), ACT.Tanh),
                                 (tok["qk", p],), ma)

        def scores(p):
            r, k = p % RING, p % 2
            a = VE.put(lambda e: e.tensor_tensor(ephi[:, k], slot[:, r, :, ROW:ROW + A], spread(phi[:, :], PAIR, A), ALU.mult),
                       some(tok["e", p], tok.get(("score", p - 2))), mv)
            tok["ephi", p] = a

        def scores2(p):
            k = p % 2
            tok["score", p] = VE.put(lambda e: e.tensor_reduce(score[:, p * PAIR:(p + 1) * PAIR], ephi[:, k], AX.X, ALU.add),
                                     (tok["ephi", p],), mv)
            tok["exp", p] = AC.put(lambda e: e.activation(wexp[:, p % 4, :], score[:, p * PAIR:(p + 1) * PAIR], ACT.Exp, bias=NSHIFT),
                                   some(tok["score", p], tok.get(("ohw", p - 4))), ma)

        def weigh(p):
            for j in range(PAIR):
                t = p * PAIR + j
                tok["ohw", p] = VE.put(lambda e, t=t, j=j: e.tensor_scalar(ohw[:, p % 3, j, :], row1[:, :], lof[:, t:t + 1], wexp[:, p % 4, j:j + 1],
                                                                          ALU.is_equal, ALU.mult),
                                       some(tok["exp", p], tok.get(("sum", p - 3))), mv)

        def total(p):
            M, r = SM[p % 2], p % RING
            for j in range(PAIR):
                tok["sum", p] = PE.put(lambda e, j=j: e.matmul(M[:, 0:SUMS], ohw[:, p % 3, j, :], slot[:, r, j, A:SLOT], start=j == 0, stop=j == PAIR - 1),
                                       some(tok["ohw", p], tok.get(("acc", p - 2))), mp)

        def accumulate(p):
            if p % PAIRS_PER_CHUNK == 0:
                load_blocks(VE, "ve_block", 1, p // PAIRS_PER_CHUNK)

            def build(e):
                b = e.snap(regs["ve_block"][p % PAIRS_PER_CHUNK], min_val=0, max_val=(NB - 1) * SUMS)
                return e.tensor_tensor(sums[:, bass.ds(b, SUMS)], sums[:, bass.ds(b, SUMS)], SM[p % 2][:, 0:SUMS], ALU.add)
            tok["acc", p] = VE.put(build, some(tok["sum", p], tok.get(("acc", p - 1)), z1, z2, z3), mv)

        sure_pairs = -(-E // (PAIR * PARTS))
        NC = NP // PAIRS_PER_CHUNK
        FIRST_ASKED = min(NC, -(-sure_pairs // PAIRS_PER_CHUNK) + 1)
        parts_of_pass = {k: [] for k in Q}
        landed_at = []

        def cut():
            for k, q in Q.items():
                parts_of_pass[k].append(q.items)
                q.items = []
            landed_at.append([(c, c.value) for c in mg])

        z4 = VE.put(lambda e: e.memset(score[:, (FIRST_ASKED - 1) * CHUNK:NTS], -1e30), (), mv) if FIRST_ASKED < NC else None
        STAGES = [(gather, 0), (turn, 1), (qk, 2), (scores, 3), (total, 5), (scores2, 3), (accumulate, 6), (weigh, 4)]
        for p in range(NP + 6):
            if p == NP or p < NP and p % PAIRS_PER_CHUNK == 0 and p // PAIRS_PER_CHUNK >= FIRST_ASKED:
                cut()
            if p < NP and p % PAIRS_PER_CHUNK == 0:
                onehots(p // PAIRS_PER_CHUNK)
            for stage, lag in STAGES:
                if 0 <= p - lag < NP:
                    stage(p - lag)
        cut()
        over = {k: sem(f"steps_over_{k}") for k in Q}
        ev, ep, ea = sem("end_vector"), sem("end_pool"), sem("end_scalar")
        for k, q in Q.items():
            q.put(lambda e: e.drain(), (), over[k])
        for k, q in Q.items():
            q.put(None, [(c, 1) for j, c in over.items() if j != k])
        VE.put(lambda e: e.tensor_reduce(RMAX, score[:, :], AX.X, ALU.max), (), ev)
        m1 = PO.put(lambda e: e.partition_all_reduce(GMAX, RMAX, PARTS, bass.bass_isa.ReduceOp.max), [(ev, ev.value)], ep)
        AC.put(lambda e: e.activation(TMP, GMAX, ACT.Exp, bias=NSHIFT), (m1,), ea)
        VE.put(lambda e: e.tensor_scalar(EPS9, TMP, 1e-9, None, ALU.mult), [(ea, ea.value)], ev)
        VE.put(lambda e: e.tensor_scalar(NSHIFT, GMAX, -1.0, None, ALU.mult), [(ev, ev.value)], ev)
        for k, q in Q.items():
            parts_of_pass[k].append(q.items)
        for q in Q.values():
            q.items, q.reached = [], {}
        arrive = {k: sem(f"pass_over_{k}") for k in Q if k != "sync"}
        leave = {k: sem(f"pass_next_{k}") for k in Q if k != "sync"}
        pass_sems = [mv, mp, ma, mgp, *mg, ev, ep, ea, *over.values()]

        lists.close()
        fin = scope()
        FB = 2
        FX, FR = 4, 3
        fx = sb(fin, "x_again", [PARTS, FX, FB, D], f32)
        tT = sb(fin, "sums_T", [PARTS, 2, FB, 2, PARTS], f32)
        rden = sb(fin, "one_over_weight", [PARTS, NB], f32)
        hres = sb(fin, "residual", [PARTS, FR, FB, D], f32)
        bst = sb(fin, "bn_stats", [PARTS, FR, FB, 6], f32)
        mvar = sb(fin, "mean_var", [PARTS, FR, FB, 2], f32)
        sd = sb(fin, "deviation", [PARTS, FR, 2, FB], f32)
        fo = sb(fin, "out_rows", [PARTS, 2, FB, D], f32)
        sv = sums[:, :].rearrange("p (b s) -> p b s", s=SUMS)
        V(lambda e: e.tensor_scalar(rden[:, :], sv[:, :, SUMS - 1], EPS9, None, ALU.add))
        V(lambda e: e.reciprocal(rden[:, :], rden[:, :]))
        eps = V(lambda e: e.memset(TMP, 1e-5))
        fl = [sem(f"x_again_loaded_{i}") for i in range(FX)]
        fs = [sem(f"out_stored_{i}") for i in range(2)]
        TT, NUM = [bank[0], bank[1]], [bank[2], bank[3]]
        TE = A + 1
        f_ = {}

        def split(i):
            b0 = i * FB
            n = min(FB, NB - b0)
            return b0, n, n if b0 + n < NB or LAST == PARTS else n - 1

        def f_load(i):
            b0, n, whole = split(i)
            k = i % FX
            w_ = some(f_.get(("res", i - FX)))
            if whole < n:
                w_ = [VE.put(lambda e: e.memset(fx[:, k, whole, :], 0.0), w_, ve)]
            if whole:
                f_["x", i] = SP.put(lambda e: e.dma_start(
                    fx[:, k, 0:whole, :], x[b0 * PARTS:(b0 + whole) * PARTS, :].rearrange("(b p) d -> p b d", p=PARTS)), w_, fl[k], 16)
            if whole < n:
                f_["x", i] = SP.put(lambda e: e.dma_start(fx[0:LAST, k, whole, :], x[(NB - 1) * PARTS:N, :]), w_, fl[k], 16)

        def f_turn(i):
            b0, n, _ = split(i)
            s = i % 2
            for j in range(n):
                PE.put(lambda e, j=j: e.transpose(TT[s][:, j * 256:j * 256 + PARTS], sv[:, b0 + j, 0:D], identf[:, :]), some(f_.get(("tT", i - 2))), pe)
                t = PE.put(lambda e, j=j: e.transpose(TT[s][0:TE, j * 256 + PARTS:(j + 1) * 256], sv[:, b0 + j, D:SUMS], identf[:, :]), (), pe)
            ttv = TT[s][:, 0:n * 256].rearrange("p (j a c) -> p j a c", a=2, c=PARTS)
            AC.put(lambda e: e.activation(tT[:, s, 0:n, 0, :], ttv[:, :, 0, :], ACT.Copy), some(t, f_.get(("num", i - 2))), ac)
            f_["tT", i] = AC.put(lambda e: e.activation(tT[0:TE, s, 0:n, 1, :], ttv[0:TE, :, 1, :], ACT.Copy), (), ac)

        def f_product(i):
            b0, n, _ = split(i)
            s = i % 2
            for j in range(n):
                o = NUM[s][:, j * D:(j + 1) * D]
                PE.put(lambda e, j=j, o=o: e.matmul(o, tT[:, s, j, 0, :], wy[:, :], start=True, stop=False), some(f_["tT", i], f_.get(("res", i - 2))), pe)
                f_["num", i] = PE.put(lambda e, j=j, o=o: e.matmul(o, tT[0:TE, s, j, 1, :], web[:, :], start=False, stop=True), (), pe)

        def f_residual(i):
            b0, n, _ = split(i)
            s, r, k = i % 2, i % FR, i % FX
            for j in range(n):
                f_["res", i] = VE.put(lambda e, j=j: e.scalar_tensor_tensor(
                    hres[:, r, j, :], NUM[s][:, j * D:(j + 1) * D], rden[:, b0 + j:b0 + j + 1], fx[:, k, j, :], ALU.mult, ALU.add),
                    some(f_["num", i], f_["x", i], eps, f_.get(("out", i - FR))), ve)

        def f_stats(i):
            b0, n, _ = split(i)
            r = i % FR
            for j in range(n):
                a = VE.put(lambda e, j=j: e.bn_stats(bst[:, r, j, :], hres[:, r, j, :]), some(f_["res", i], f_.get(("sd", i - FR))), ve)
            f_["bn", i] = a

        def f_aggregate(i):
            b0, n, _ = split(i)
            r = i % FR
            for j in range(n):
                a = VE.put(lambda e, j=j: e.bn_aggr(mvar[:, r, j, :], bst[:, r, j, :]), (f_["bn", i],), ve)
            f_["sd", i] = AC.put(lambda e: e.activation(sd[:, r, 0, 0:n], mvar[:, r, 0:n, 1], ACT.Sqrt, bias=TMP), (a,), ac)

        def f_invert(i):
            b0, n, _ = split(i)
            r = i % FR
            f_["inv", i] = VE.put(lambda e: e.reciprocal(sd[:, r, 1, 0:n], sd[:, r, 0, 0:n]), (f_["sd", i],), ve)

        def f_norm(i):
            b0, n, whole = split(i)
            s, r = i % 2, i % FR
            for j in range(n):
                b_ = f_["out", i] = VE.put(lambda e, j=j: e.tensor_scalar(
                    fo[:, s, j, :], hres[:, r, j, :], mvar[:, r, j, 0:1], sd[:, r, 1, j:j + 1],
                    ALU.subtract, ALU.mult), some(f_["inv", i], f_.get(("stored", i - 2))), ve)
            if whole:
                f_["stored", i] = SP.put(lambda e: e.dma_start(
                    out[b0 * PARTS:(b0 + whole) * PARTS, :].rearrange("(b p) d -> p b d", p=PARTS), fo[:, s, 0:whole, :]), (b_,), fs[s], 16)
            if whole < n:
                f_["stored", i] = SP.put(lambda e: e.dma_start(out[(NB - 1) * PARTS:N, :], fo[0:LAST, s, whole, :]), (b_,), fs[s], 16)

        NF = -(-NB // FB)
        F_STAGES = [(f_load, 0), (f_turn, 2), (f_product, 3), (f_invert, 5), (f_stats, 4), (f_residual, 3), (f_norm, 5), (f_aggregate, 4)]
        for i in range(NF + 5):
            for stage, lag in F_STAGES:
                if 0 <= i - lag < NF:
                    stage(i - lag)
        SP.put(None, [(c, c.value) for c in fs])
        after_pass = {k: q.items for k, q in Q.items()}

        def play(name, engine):
            q = Queue()
            q.items = before_pass[name]
            q.run(engine)
            reg = engine.alloc_register(f"passes_{name}")
            engine.reg_load(reg, passes[0:1, 0:1])
            used_reg = engine.alloc_register(f"pairs_used_{name}")
            engine.reg_load(used_reg, used[0:1, 0:1])
            pairs_used = engine.snap(used_reg, min_val=0, max_val=NP)
            with engine.Fori(0, engine.snap(reg, min_val=1, max_val=2)):
                first, *asked, flush, end = parts_of_pass[name]

                def run(items):
                    q.items = items
                    q.run(engine)

                def landed(at):
                    if name == "gpsimd":
                        for c, value in landed_at[at]:
                            if value:
                                engine.wait_ge(c.sem, value)

                def steps(i):
                    if i == len(asked):
                        run(flush)
                        landed(i + 1)
                        return
                    with engine.If(pairs_used > (FIRST_ASKED + i - 1) * PAIRS_PER_CHUNK):
                        run(asked[i])
                        steps(i + 1)
                    if name == "gpsimd":
                        with engine.Else():
                            landed(i)

                run(first)
                steps(0)
                run(end)
                if name == "sync":
                    for c in arrive.values():
                        engine.wait_ge(c.sem, 1)
                    for c in (*arrive.values(), *pass_sems):
                        engine.sem_clear(c.sem)
                    for c in leave.values():
                        engine.sem_inc(c.sem, 1)
                else:
                    if name == "gpsimd":
                        engine.dma_reset()
                    engine.drain().then_inc(arrive[name].sem, 1)
                    engine.wait_ge(leave[name].sem, 1)
                    engine.sem_inc(leave[name].sem, -1)
            q.items = after_pass[name]
            q.run(engine)

        block = ctx.enter_context(nc.Block())

        @block.sync
        def _(e):
            play("sync", e)

        @block.gpsimd
        def _(e):
            play("gpsimd", e)

        @block.vector
        def _(e):
            play("vector", e)

        @block.scalar
        def _(e):
            play("scalar", e)

        @block.tensor
        def _(e):
            play("tensor", e)
        fin.close()
        main.close()


_INS = ["x", "src", "dst", "L0_gnn_Wq", "L0_gnn_Wk", "L0_gnn_Wphi", "L0_gnn_Wy_w", "L0_gnn_Wy_b", "L0_gnn_We"]


def kernel(**inputs):
    import numpy as np
    import concourse.bacc as bacc
    from concourse.bass_utils import run_bass_kernel_spmd

    nc = bacc.Bacc("TRN2", target_bir_lowering=False, num_devices=1)
    arrays, args = {}, []
    for name in _INS:
        a = np.ascontiguousarray(inputs[name])
        arrays[f"in_{name}"] = a
        args.append(nc.dram_tensor(f"in_{name}", a.shape, mybir.dt.from_np(a.dtype), kind="ExternalInput").ap())
    shape = arrays["in_x"].shape
    args.append(nc.dram_tensor("out", shape, mybir.dt.float32, kind="ExternalOutput").ap())
    gnn_program(nc, *args)
    r = run_bass_kernel_spmd(nc, [arrays], core_ids=[0])
    return r.results[0]["out"]
```
